# Optimizing a Trainium2 kernel written in Bass

```python
import numpy as np
import jax
import jax.numpy as jnp

def _softmax(x, axis=-1):
    return jax.nn.softmax(x, axis=axis)

def _gelu(x):
    return jax.nn.gelu(x, approximate=True)

def _silu(x):
    return jax.nn.silu(x)

def _sigmoid(x):
    return jax.nn.sigmoid(x)

def _layernorm(x, axis=-1, eps=1e-05):
    m = jnp.mean(x, axis=axis, keepdims=True)
    v = jnp.var(x, axis=axis, keepdims=True)
    return (x - m) / jnp.sqrt(v + eps)

def _scatter_add(tgt, idx, src, axis=0):
    return tgt.at[idx].add(src)

def _segment_sum(src, seg, n):
    return jax.ops.segment_sum(src, seg, n)
kernel_name = 'mk_xattn_ffn_d1_seqx_r4_c453dc'

def setup_inputs(seed: int=0):
    np.random.seed(seed)
    _w = jnp.asarray

    def _rec_inputs():
        import jax
        import jax.numpy as jnp
        _rk = jax.random.key(seed)
        x = -0.0003929 + 0.9999 * jax.random.normal(jax.random.fold_in(_rk, 1), (16, 128, 1024), jnp.float32)
        _lenS = 128 - jax.random.randint(jax.random.fold_in(_rk, 7), (16,), 0, max(1, 128 // 4) + 1, jnp.int32)
        _lenS2 = 128 - jax.random.randint(jax.random.fold_in(_rk, 8), (16,), 0, max(1, 128 // 4) + 1, jnp.int32)
        _ctx_4096P = jax.random.normal(jax.random.fold_in(_rk, 11), (16, 16, 1024), jnp.float32)
        _ctx_4096c = jax.random.dirichlet(jax.random.fold_in(_rk, 511), 0.3 * jnp.ones((16,), jnp.float32), (16, 128))
        _ctx_4096t = jnp.einsum('bsk,bkd->bsd', _ctx_4096c, _ctx_4096P)
        _ctx_4096t = _ctx_4096t * jax.lax.rsqrt(jnp.mean(jnp.square(_ctx_4096t)) + 1e-12) * 0.953939
        ctx_4096 = 2.81802e-05 + 1.00001 * (_ctx_4096t + 0.3 * jax.random.normal(jax.random.fold_in(_rk, 611), (16, 128, 1024), jnp.float32))
        return (x, ctx_4096)
    x, ctx_4096 = _rec_inputs()

    def _L0_xattn_setup():
        import jax, jax.numpy as jnp
        import numpy as np
        DIM = 128
        HEADS = 8
        DIM_HEAD = 64
        HIDDEN = HEADS * DIM_HEAD
        SCALE = DIM_HEAD ** (-0.5)
        key = jax.random.key(seed)
        ks = jax.random.split(key, 9)
        b, n = (8, 1024)
        std = 1.0 / np.sqrt(DIM)
        return {'q': jax.random.normal(ks[0], (b, DIM, n), jnp.float32), 'k': jax.random.normal(ks[1], (b, DIM, n), jnp.float32), 'v': jax.random.normal(ks[2], (b, DIM, n), jnp.float32), 'Wq': jax.random.normal(ks[3], (HIDDEN, DIM), jnp.float32) * std, 'Wk': jax.random.normal(ks[4], (HIDDEN, DIM), jnp.float32) * std, 'Wv': jax.random.normal(ks[5], (HIDDEN, DIM), jnp.float32) * std, 'Wo': jax.random.normal(ks[6], (DIM, HIDDEN), jnp.float32) * (1.0 / np.sqrt(HIDDEN)), 'bo': jax.random.normal(ks[7], (DIM,), jnp.float32) * 0.01, 'g': jnp.ones((1, DIM, 1), jnp.float32)}
    _L0_xattn_all = _L0_xattn_setup()
    _L0_xattn_in = {k: v for k, v in _L0_xattn_all.items() if k in ('Wq', 'Wk', 'Wv', 'Wo', 'bo', 'g')}
    del _L0_xattn_all

    def _L0_ffn_setup():
        import jax, jax.numpy as jnp
        import numpy as np
        B, S, IN, OUT = (4, 512, 1024, 1024)

        def _dequant_weight(qweight, scales, zeros):
            low = qweight & 15
            high = qweight >> 4 & 15
            w_int = jnp.stack([low, high], axis=1).reshape(-1, qweight.shape[1])
            zp = jnp.round(zeros / scales)
            return (w_int.astype(jnp.float32) - zp.T) * scales.T
        key = jax.random.key(seed)
        k_x, k_q, k_s, k_z, k_b = jax.random.split(key, 5)
        x = jax.random.normal(k_x, (B, S, IN), dtype=jnp.float32)
        qweight = jax.random.randint(k_q, (IN // 2, OUT), 0, 64, dtype=jnp.int32)
        scales = jax.random.uniform(k_s, (OUT, 1), minval=0.01, maxval=0.05, dtype=jnp.float32)
        zeros = jax.random.normal(k_z, (OUT, 1), dtype=jnp.float32) * 0.1
        bias = jax.random.normal(k_b, (OUT,), dtype=jnp.float32) * 0.02
        return {'x': x, 'qweight': qweight, 'scales': scales, 'zeros': zeros, 'bias': bias}
    _L0_ffn_all = _L0_ffn_setup()
    _L0_ffn_in = {k: v for k, v in _L0_ffn_all.items() if k in ('qweight', 'scales', 'zeros', 'bias')}
    del _L0_ffn_all
    return {'x': x, 'ctx_4096': ctx_4096, 'L0_xattn_Wq': _L0_xattn_in['Wq'], 'L0_xattn_Wk': _L0_xattn_in['Wk'], 'L0_xattn_Wv': _L0_xattn_in['Wv'], 'L0_xattn_Wo': _L0_xattn_in['Wo'], 'L0_xattn_bo': _L0_xattn_in['bo'], 'L0_xattn_g': _L0_xattn_in['g'], 'L0_ffn_qweight': _L0_ffn_in['qweight'], 'L0_ffn_scales': _L0_ffn_in['scales'], 'L0_ffn_zeros': _L0_ffn_in['zeros'], 'L0_ffn_bias': _L0_ffn_in['bias']}

def reference(x, ctx_4096, L0_xattn_Wq, L0_xattn_Wk, L0_xattn_Wv, L0_xattn_Wo, L0_xattn_bo, L0_xattn_g, L0_ffn_qweight, L0_ffn_scales, L0_ffn_zeros, L0_ffn_bias):
    import jax
    import jax.numpy as jnp

    def _L0_xattn_ref(q, k, v, Wq, Wk, Wv, Wo, bo, g):
        import jax, jax.numpy as jnp
        import numpy as np
        DIM = 128
        HEADS = 8
        DIM_HEAD = 64
        HIDDEN = HEADS * DIM_HEAD
        SCALE = DIM_HEAD ** (-0.5)
        b = q.shape[0]
        qh = jnp.einsum('bcn,oc->bon', q, Wq).reshape(b, HEADS, DIM_HEAD, -1)
        kh = jnp.einsum('bcn,oc->bon', k, Wk).reshape(b, HEADS, DIM_HEAD, -1)
        vh = jnp.einsum('bcn,oc->bon', v, Wv).reshape(b, HEADS, DIM_HEAD, -1)
        qh = jax.nn.softmax(qh, axis=-2) * SCALE
        kh = jax.nn.softmax(kh, axis=-1)
        context = jnp.einsum('bhdn,bhen->bhde', kh, vh)
        out = jnp.einsum('bhde,bhdn->bhen', context, qh)
        out = out.reshape(b, HIDDEN, -1)
        out = jnp.einsum('bcn,oc->bon', out, Wo) + bo[None, :, None]
        norm = jnp.maximum(jnp.sqrt(jnp.sum(out * out, axis=1, keepdims=True)), 1e-12)
        return out / norm * g * np.sqrt(DIM)

    def _L0_ffn_ref(x, qweight, scales, zeros, bias):
        import jax, jax.numpy as jnp
        import numpy as np
        B, S, IN, OUT = (4, 512, 1024, 1024)

        def _dequant_weight(qweight, scales, zeros):
            low = qweight & 15
            high = qweight >> 4 & 15
            w_int = jnp.stack([low, high], axis=1).reshape(-1, qweight.shape[1])
            zp = jnp.round(zeros / scales)
            return (w_int.astype(jnp.float32) - zp.T) * scales.T
        w = _dequant_weight(qweight, scales, zeros)
        y = jnp.einsum('bsi,io->bso', x.astype(jnp.float32), w) + bias
        return y.astype(x.dtype)
    x = x + _L0_xattn_ref(_layernorm(x, axis=-1), ctx_4096, ctx_4096, L0_xattn_Wq, L0_xattn_Wk, L0_xattn_Wv, L0_xattn_Wo, L0_xattn_bo, L0_xattn_g)
    x = x + _L0_ffn_ref(_layernorm(x, axis=-1), L0_ffn_qweight, L0_ffn_scales, L0_ffn_zeros, L0_ffn_bias)
    return x

_drawn_inputs = setup_inputs


def setup_inputs(seed=0):
    import zlib

    import numpy as np

    out = dict(_drawn_inputs(seed))
    spreads = {'L0_xattn_g': (1.0, 0.2)}
    factors = {'L0_ffn_zeros': 8.0, 'L0_ffn_bias': 8.0}
    for name, (base, spread) in spreads.items():
        noise = np.random.default_rng([zlib.crc32(name.encode()), seed]).standard_normal(out[name].shape)
        drawn = base * np.exp(spread * noise) if base else spread * noise
        out[name] = jnp.asarray(drawn.astype(out[name].dtype))
    for name, factor in factors.items():
        out[name] = (out[name] * factor).astype(out[name].dtype)
    return out
```

```python
from contextlib import ExitStack

import numpy as np

import concourse.bass as bass
from concourse import mybir

F32 = mybir.dt.float32
F32R = mybir.dt.float32r
F16 = mybir.dt.float16
I32 = mybir.dt.int32
ALU = mybir.AluOpType
ACT = mybir.ActivationFunctionType
AX_X = mybir.AxisListType.X

P = 128
BANK = 512
STEPS = 8
LN_EPS = 1e-5
NORM_FLOOR_SQ = 1e-24
ROUND = 1.5 * 2.0 ** 23


def build(nc, x, ctx_in, wq, wk, wv, wo, bo, g, qweight, scales, zeros, bias, out):
    NB, DIM, N = x.shape
    HID = wq.shape[0]
    DH = 64
    HEADS = HID // DH
    HC = HID // P
    TC = N // P
    HALVES = N // BANK
    OUT = qweight.shape[1]
    RC = qweight.shape[0] // P
    assert DIM == P and TC == STEPS and HC == 4 and OUT == N and 2 * RC == TC
    q_scale = DH ** -0.5
    g_scale = float(np.sqrt(DIM))

    with ExitStack() as ctx:
        def sb(name, shape, dt=F32):
            return ctx.enter_context(nc.sbuf_tensor(name, shape, dt))

        def psum(name, shape):
            return ctx.enter_context(nc.psum_tensor(name, shape, F32))

        def sem(name):
            return ctx.enter_context(nc.semaphore(name))

        ident = sb("ident", [P, P])
        ones = sb("ones", [P, 1])
        neg_half = sb("neg_half", [P, TC])
        eps_col = sb("eps_col", [P, 1])
        minus_col = sb("minus_col", [P, 1])
        wq_hi = sb("wq_hi", [P, HID], F32R)
        wq_lo = sb("wq_lo", [P, HID], F32R)
        wk_hi = sb("wk_hi", [P, HID], F32R)
        wk_lo = sb("wk_lo", [P, HID], F32R)
        vo = sb("vo", [P, HEADS * P])
        w_int = sb("w_int", [P, 2, RC, OUT], F16)
        scale_bc = sb("scale_bc", [P, OUT])
        zero_bc = sb("zero_bc", [P, OUT])
        bias_bc = sb("bias_bc", [P, OUT])
        bo_col = sb("bo_col", [P, 1])
        gs_col = sb("gs_col", [P, 1])
        bogs_col = sb("bogs_col", [P, 1])

        x_in = [sb(f"x_in{s}", [P, N]) for s in range(2)]
        c_in = [sb(f"c_in{s}", [P, N]) for s in range(2)]
        x_res = sb("x_res", [P, N])
        xn = sb("xn", [P, N])
        xn_hi = [sb(f"xn_hi{s}", [P, N], F32R) for s in range(2)]
        xn_lo = [sb(f"xn_lo{s}", [P, N], F32R) for s in range(2)]
        c_hi = sb("c_hi", [P, N], F32R)
        c_lo = sb("c_lo", [P, N], F32R)
        c_t = [sb(f"c_t{s}", [P, TC, P]) for s in range(2)]
        stats1 = sb("stats1", [P, 2, 6])
        mv1 = sb("mv1", [P, 2])
        ve1 = sb("ve1", [P, 1])
        rstd1 = sb("rstd1", [P, 1])
        QR = 4
        q_exp = sb("q_exp", [P, QR, HID])
        q_nmax = sb("q_nmax", [P, QR, HEADS])
        q_sum = sb("q_sum", [P, QR, HEADS])
        q_rec = sb("q_rec", [P, QR, HEADS])
        k_exp = sb("k_exp", [P, 2, N])
        k_nmax = sb("k_nmax", [P, HC])
        k_sum = sb("k_sum", [P, 2, HC])
        k_rec = sb("k_rec", [P, HC])
        k_t = sb("k_t", [P, TC, HID])
        q_t = [sb(f"q_t{s}", [P, HC, N]) for s in range(2)]
        m_t = sb("m_t", [P, HID])
        g_t = sb("g_t", [P, HC, P])
        og = sb("og", [P, N])
        sq = sb("sq", [P, N])
        n2 = sb("n2", [P, TC])
        rn = sb("rn", [P, TC])
        att = sb("att", [P, N])
        x2 = sb("x2", [P, N])
        stats2 = sb("stats2", [P, 2, 6])
        mv2 = sb("mv2", [P, 2])
        ve2 = sb("ve2", [P, 1])
        rstd2 = sb("rstd2", [P, 1])
        mr2 = sb("mr2", [P, 1])
        nmr2 = sb("nmr2", [P, 1])
        rs2 = sb("rs2", [P, 1])
        nrs2 = sb("nrs2", [P, 1])
        x2n = sb("x2n", [P, 2, RC * P])
        x2b = sb("x2b", [P, N])
        x2_hi = sb("x2_hi", [P, TC, P], F16)
        x2_lo = sb("x2_lo", [P, TC, P], F16)
        y = sb("y", [P, OUT])

        q_packed = q_t[0][:].bitcast(I32).rearrange("p c n -> p (c n)").rearrange("p (m o) -> p m o", m=RC)
        q_nibble = q_t[1][:].bitcast(I32).rearrange("p c n -> p (c n)").rearrange("p (m o) -> p m o", m=RC)
        k_flat = k_t[:].rearrange("p t h -> p (t h)")
        wq_in = k_flat[:, 0:HID].rearrange("p (k c) -> p k c", k=HC)
        wk_in = k_flat[:, HID:2 * HID].rearrange("p (k c) -> p k c", k=HC)
        wv_in = k_flat[:, 2 * HID:3 * HID].rearrange("p (k c) -> p k c", k=HC)
        wo_in = k_flat[:, 3 * HID:4 * HID]
        wo_t = k_flat[:, 4 * HID:5 * HID].rearrange("p (k o) -> p k o", k=HC)
        wq_tf = k_flat[:, 5 * HID:6 * HID]
        wk_tf = k_flat[:, 6 * HID:7 * HID]

        ps_q = psum("ps_q", [P, BANK])
        ps_k = psum("ps_k", [P, HALVES * BANK])
        ps_tq = psum("ps_tq", [P, BANK])
        ps_tk = psum("ps_tk", [P, BANK])
        ps_m = psum("ps_m", [P, BANK])
        ps_o = [psum(f"ps_o{h}", [P, BANK]) for h in range(2)]

        w_loaded = sem("w_loaded")
        consts_made = sem("consts_made")
        gs_done = sem("gs_done")
        set_dve = sem("set_dve")
        set_pe = sem("set_pe")
        x_loaded = [sem(f"x_loaded{s}") for s in range(2)]
        c_loaded = [sem(f"c_loaded{s}") for s in range(2)]
        xres_loaded = sem("xres_loaded")
        y_stored = sem("y_stored")
        stats1_part = sem("stats1_part")
        stats1_done = sem("stats1_done")
        ve1_done = sem("ve1_done")
        rstd1_done = sem("rstd1_done")
        xn_done = sem("xn_done")
        xnhi_done = sem("xnhi_done")
        xnlo_done = sem("xnlo_done")
        chi_done = sem("chi_done")
        clo_done = sem("clo_done")
        q_ready = sem("q_ready")
        k_ready = sem("k_ready")
        qmax_done = sem("qmax_done")
        qsub_done = sem("qsub_done")
        qexp_done = sem("qexp_done")
        qsum_done = sem("qsum_done")
        qrec_done = sem("qrec_done")
        qs_done = sem("qs_done")
        tq_ready = sem("tq_ready")
        tq_moved = sem("tq_moved")
        kmax_done = sem("kmax_done")
        kexp_done = sem("kexp_done")
        tk_ready = sem("tk_ready")
        tk_moved = sem("tk_moved")
        tc_ready = sem("tc_ready")
        tc_moved = sem("tc_moved")
        m_ready = sem("m_ready")
        m_moved = sem("m_moved")
        krec_done = sem("krec_done")
        g_ready = sem("g_ready")
        g_moved = sem("g_moved")
        out_ready = sem("out_ready")
        og_done = sem("og_done")
        sq_done = sem("sq_done")
        n2_ready = sem("n2_ready")
        n2_moved = sem("n2_moved")
        rn_done = sem("rn_done")
        rb_ready = sem("rb_ready")
        att_done = sem("att_done")
        x2_done = sem("x2_done")
        stats2_part = sem("stats2_part")
        stats2_done = sem("stats2_done")
        rstd2_steps = sem("rstd2_steps")
        x2n_done = sem("x2n_done")
        nrs_done = sem("nrs_done")
        x2b_done = sem("x2b_done")
        x2c_done = sem("x2c_done")
        tx_ready = sem("tx_ready")
        x2hi_done = sem("x2hi_done")
        x2lo_done = sem("x2lo_done")
        y_ready = sem("y_ready")
        ymul_done = sem("ymul_done")
        y_done = sem("y_done")

        def begun(value):
            return not isinstance(value, int) or value > 0

        def loads(b, s):
            return 8 * (b - s) + 16

        FIRST, LAST = -1, NB + 2
        LOOP = (3, NB - 1)

        def pipeline(eng, iteration, end=LOOP[1]):
            def peeled(i):
                iteration(i, i % 2, i + 1 < NB, 0 <= i < NB, 0 <= i - 1 < NB, 0 <= i - 2 < NB)

            for i in range(FIRST, LOOP[0]):
                peeled(i)
            with eng.Fori(LOOP[0], end, 2) as i:
                iteration(i, LOOP[0] % 2, True, True, True, True)
                iteration(i + 1, (LOOP[0] + 1) % 2, True, True, True, True)
            for i in range(end, LAST):
                peeled(i)

        def halves(ap):
            return [ap[:, h * BANK:(h + 1) * BANK] for h in range(HALVES)]

        block = ctx.enter_context(nc.Block())

        @block.sync
        def _(sp):
            for dst, src in (
                (wq_in, wq.rearrange("(k p) c -> p k c", p=P)),
                (wk_in, wk.rearrange("(k p) c -> p k c", p=P)),
                (wv_in, wv.rearrange("(k p) c -> p k c", p=P)),
                (wo_in, wo),
                (bo_col[:], bo.rearrange("(p a) -> p a", a=1)),
                (gs_col[:], g.rearrange("a p b -> (a p) b")),
                (scale_bc[:], scales.rearrange("n a -> a n").to_broadcast([P, OUT])),
                (zero_bc[:], zeros.rearrange("n a -> a n").to_broadcast([P, OUT])),
                (bias_bc[:], bias.rearrange("(a n) -> a n", a=1).to_broadcast([P, OUT])),
                (q_packed, qweight.rearrange("(m p) o -> p m o", p=P)),
            ):
                sp.dma_start(dst, src).then_inc(w_loaded, 16)

            def load(b, s):
                sp.dma_start(x_in[s][:], x[b]).then_inc(x_loaded[s], 16)
                sp.dma_start(c_in[s][:], ctx_in[b]).then_inc(c_loaded[s], 16)

            load(0, 0)
            load(1, 1)

            def kept(value):
                return value if isinstance(value, int) else sp.snap(value)

            def iteration(i, s, do_n, do_a, do_c, do_f):
                c, f = i - 1, i - 2
                if do_c:
                    before = kept(c)
                    sp.wait_ge(w_loaded, 160)
                    if begun(c):
                        sp.wait_ge(x2_done, before)
                    sp.dma_start(x_res[:], x[c]).then_inc(xres_loaded, 16)
                if not isinstance(i, int) or 0 <= i < NB - 2:
                    after, twice = kept(i + 1), kept(2 * (i + 1))
                    sp.wait_ge(w_loaded, 160)
                    sp.wait_ge(xn_done, after)
                    sp.dma_start(x_in[s][:], x[i + 2]).then_inc(x_loaded[s], 16)
                    sp.wait_ge(w_loaded, 160)
                    sp.wait_ge(chi_done, after)
                    sp.wait_ge(clo_done, after)
                    sp.wait_ge(tc_ready, twice)
                    sp.dma_start(c_in[s][:], ctx_in[i + 2]).then_inc(c_loaded[s], 16)
                if do_f:
                    finished = kept(2 * (f + 1))
                    sp.wait_ge(w_loaded, 160)
                    sp.wait_ge(y_done, finished)
                    sp.dma_start(out[f], y[:]).then_inc(y_stored, 16)

            pipeline(sp, iteration, end=NB - 3)
            sp.wait_ge(y_stored, 16 * NB)

        @block.gpsimd
        def _(pool):
            nc.gpsimd.memset(ident[:], 0.0).then_inc(consts_made, 1)
            nc.gpsimd.memset(ones[:], 1.0).then_inc(consts_made, 1)
            nc.gpsimd.memset(neg_half[:], -0.5).then_inc(consts_made, 1)
            nc.gpsimd.memset(eps_col[:], LN_EPS).then_inc(consts_made, 1)
            nc.gpsimd.memset(minus_col[:], -1.0).then_inc(consts_made, 1)
            pool.wait_ge(consts_made, 5)
            nc.gpsimd.affine_select(out=ident[:], in_=ident[:], compare_op=ALU.not_equal, fill=1.0,
                                    base=0, pattern=[[-1, P]], channel_multiplier=1).then_inc(consts_made, 1)

            def iteration(i, s, do_n, do_a, do_c, do_f):
                n, a, c, f = i + 1, i, i - 1, i - 2

                def scale_q(j):
                    r = j % QR
                    pool.wait_ge(qrec_done, 8 * a + j + 1)
                    chunk = q_exp[:, r, :].rearrange("p (h d) -> p h d", h=HEADS)
                    rec = q_rec[:, r, :].unsqueeze(2).to_broadcast([P, HEADS, DH])
                    nc.gpsimd.tensor_tensor(chunk, chunk, rec, ALU.mult).then_inc(qs_done, 1)

                for j in range(STEPS):
                    if j == 0 and do_f:
                        pool.wait_ge(n2_moved, f + 1)
                        nc.gpsimd.tensor_tensor(rn[:], n2[:], neg_half[:], ALU.pow).then_inc(rn_done, 1)
                    if j >= 1 and do_a:
                        scale_q(j - 1)
                    if j == 1 and do_f:
                        pool.wait_ge(att_done, 2 * (f + 1))
                        pool.wait_ge(xres_loaded, 16 * (f + 1))
                        if begun(f):
                            pool.wait_ge(x2c_done, f)
                        nc.gpsimd.tensor_tensor(x2[:], att[:], x_res[:], ALU.add).then_inc(x2_done, 1)
                    if j == 2 and do_f:
                        pool.wait_ge(stats2_done, f + 1)
                        nc.gpsimd.tensor_tensor(ve2[:], mv2[:, 1:2], eps_col[:], ALU.add).then_inc(rstd2_steps, 1)
                        pool.wait_ge(rstd2_steps, 4 * f + 1)
                        nc.gpsimd.tensor_tensor(rstd2[:], ve2[:], neg_half[:, 0:1], ALU.pow).then_inc(rstd2_steps, 1)
                        pool.wait_ge(rstd2_steps, 4 * f + 2)
                        nc.gpsimd.tensor_tensor(mr2[:], mv2[:, 0:1], rstd2[:], ALU.mult).then_inc(rstd2_steps, 1)
                        pool.wait_ge(rstd2_steps, 4 * f + 3)
                        nc.gpsimd.tensor_tensor(nmr2[:], mr2[:], minus_col[:], ALU.mult).then_inc(rstd2_steps, 1)
                    if j == 3 and do_f:
                        if begun(2 * f):
                            pool.wait_ge(y_done, 2 * f)
                        pool.wait_ge(x2_done, f + 1)
                        nc.gpsimd.tensor_tensor(x2b[:], x2[:], bias_bc[:], ALU.add).then_inc(x2b_done, 1)
                    if j == 4 and do_n:
                        pool.wait_ge(stats1_done, n + 1)
                        nc.gpsimd.tensor_tensor(ve1[:], mv1[:, 1:2], eps_col[:], ALU.add).then_inc(ve1_done, 1)
                        pool.wait_ge(ve1_done, n + 1)
                        nc.gpsimd.tensor_tensor(rstd1[:], ve1[:], neg_half[:, 0:1], ALU.pow).then_inc(rstd1_done, 1)
                    if j == 5 and do_n:
                        pool.wait_ge(chi_done, n + 1)
                        nc.gpsimd.tensor_tensor(c_lo[:], c_in[1 - s][:], c_hi[:].bitcast(F32),
                                                ALU.subtract).then_inc(clo_done, 1)
                    if j == 7 and do_n:
                        pool.wait_ge(xnhi_done, n + 1)
                        if begun(8 * (n - 1)):
                            pool.wait_ge(q_ready, 8 * (n - 1))
                        nc.gpsimd.tensor_tensor(xn_lo[1 - s][:], xn[:], xn_hi[1 - s][:].bitcast(F32),
                                                ALU.subtract).then_inc(xnlo_done, 1)
                if do_a:
                    scale_q(STEPS - 1)

            pipeline(pool, iteration)

        @block.scalar
        def _(act):
            act.wait_ge(w_loaded, 160)
            nc.scalar.mul(gs_col[:], gs_col[:], g_scale).then_inc(gs_done, 1)

            def iteration(i, s, do_n, do_a, do_c, do_f):
                n, a, c, f = i + 1, i, i - 1, i - 2

                def exp_k(j):
                    act.wait_ge(kmax_done, 4 * a + j + 1)
                    if begun(8 * a + 2 * (j - 2) + 2):
                        act.wait_ge(tk_ready, 8 * a + 2 * (j - 2) + 2)
                    nc.scalar.activation(k_exp[:, j % 2, :], ps_k[:], ACT.Exp, bias=k_nmax[:, j:j + 1],
                                         accum_out=k_sum[:, s, j:j + 1]).then_inc(kexp_done, 1)

                def exp_q(j):
                    act.wait_ge(qsub_done, 8 * a + j + 1)
                    nc.scalar.activation(q_exp[:, j % QR, :], q_exp[:, j % QR, :], ACT.Exp).then_inc(qexp_done, 1)

                def move_tq(b, buf, j):
                    act.wait_ge(tq_ready, 8 * b + j + 1)
                    nc.scalar.activation(q_t[buf][:, :, j * P:(j + 1) * P],
                                         ps_tq[:].rearrange("p (c t) -> p c t", c=HC),
                                         ACT.Copy).then_inc(tq_moved, 1)

                def move_tk(k):
                    t0, fc = 4 * (k % 2), k // 2
                    act.wait_ge(tk_ready, 8 * a + k + 1)
                    nc.scalar.activation(k_t[:, t0:t0 + 4, fc * P:(fc + 1) * P],
                                         ps_tk[:].rearrange("p (t c) -> p t c", t=4),
                                         ACT.Copy).then_inc(tk_moved, 1)

                for j in range(STEPS):
                    if j == 0 and do_f:
                        for h in range(HALVES):
                            act.wait_ge(out_ready, 2 * f + h + 1)
                            if h == 0:
                                if begun(f):
                                    act.wait_ge(n2_ready, f)
                                if begun(2 * f):
                                    act.wait_ge(att_done, 2 * f)
                            nc.scalar.activation(halves(sq)[h], ps_o[h][:], ACT.Square,
                                                 bias=bo_col[:]).then_inc(sq_done, 1)
                            nc.scalar.activation(halves(og)[h], ps_o[h][:], ACT.Identity, bias=bogs_col[:],
                                                 scale=gs_col[:]).then_inc(og_done, 1)
                    if 2 <= j < 6 and do_a:
                        move_tk(2 * (j - 2))
                        move_tk(2 * (j - 2) + 1)
                    if j < HC and do_a:
                        exp_k(j)
                    if do_a:
                        exp_q(j)
                    if j < 2 and do_c:
                        move_tq(c, 1 - s, 6 + j)
                    if j >= 2 and do_a:
                        move_tq(a, s, j - 2)
                    if j == 2 and do_c:
                        act.wait_ge(m_ready, c + 1)
                        nc.scalar.activation(m_t[:], ps_m[:], ACT.Copy).then_inc(m_moved, 1)
                    if j == 3 and do_f:
                        act.wait_ge(rstd2_steps, 4 * (f + 1))
                        if begun(2 * f):
                            act.wait_ge(tx_ready, 2 * f)
                        if begun(f):
                            act.wait_ge(nrs_done, f)
                        nc.scalar.activation(x2n[:], x2[:].rearrange("p (r t) -> p t r", t=2), ACT.Identity,
                                             bias=nmr2[:], scale=rstd2[:], accum_out=rs2[:]).then_inc(x2n_done, 1)
                    if j == 3 and do_a:
                        for h in range(2):
                            act.wait_ge(tc_ready, 2 * a + h + 1)
                            nc.scalar.activation(c_t[s][:, 4 * h:4 * h + 4, :],
                                                 ps_o[h][:].rearrange("p (t c) -> p t c", t=4),
                                                 ACT.Copy).then_inc(tc_moved, 1)
                    if j == 4 and do_f:
                        for h in range(2):
                            act.wait_ge(tx_ready, 2 * f + h + 1)
                            if h == 0:
                                if begun(2 * f):
                                    act.wait_ge(y_ready, 2 * f)
                            nc.scalar.activation(x2_hi[:, 4 * h:4 * h + 4, :],
                                                 ps_o[h][:].rearrange("p (t c) -> p t c", t=4),
                                                 ACT.Copy).then_inc(x2hi_done, 1)
                    if j == 4 and do_n:
                        act.wait_ge(c_loaded[1 - s], loads(n, 1 - s))
                        if begun(8 * n):
                            act.wait_ge(k_ready, 8 * n)
                        nc.scalar.activation(c_hi[:], c_in[1 - s][:], ACT.Copy).then_inc(chi_done, 1)
                    if j == 6 and do_n:
                        act.wait_ge(xn_done, n + 1)
                        if begun(8 * (n - 1)):
                            act.wait_ge(q_ready, 8 * (n - 1))
                        nc.scalar.activation(xn_hi[1 - s][:], xn[:], ACT.Copy).then_inc(xnhi_done, 1)

            pipeline(act, iteration)

        @block.vector
        def _(dve):
            dve.wait_ge(w_loaded, 160)
            steps = [0]

            def then(ins):
                ins.then_inc(set_dve, 1)
                steps[0] += 1
                dve.wait_ge(set_dve, steps[0])

            dve.wait_ge(set_pe, 1)
            for ps, full, hi, lo in ((ps_q, wq_tf, wq_hi, wq_lo), (ps_tq, wk_tf, wk_hi, wk_lo)):
                then(nc.vector.tensor_copy(full, ps[:]))
                then(nc.vector.tensor_copy(hi[:], full))
                then(nc.vector.tensor_tensor(lo[:], full, hi[:].bitcast(F32), ALU.subtract))
            then(nc.vector.tensor_copy(wo_t, ps_tk[:].rearrange("p (k o) -> p k o", k=HC)))
            dve.wait_ge(set_pe, 2)
            then(nc.vector.tensor_copy(vo[:].rearrange("p (k q o) -> p q k o", q=2, o=P),
                                       ps_k[:].rearrange("p (q k o) -> p q k o", q=2, o=P)))
            dve.wait_ge(gs_done, 1)
            then(nc.vector.tensor_tensor(bogs_col[:], bo_col[:], gs_col[:], ALU.mult))
            then(nc.vector.tensor_scalar(q_nibble, q_packed, 15, None, ALU.bitwise_and))
            then(nc.vector.tensor_copy(w_int[:, 0], q_nibble))
            then(nc.vector.tensor_scalar(q_nibble, q_packed, 4, 15, ALU.logical_shift_right, ALU.bitwise_and))
            then(nc.vector.tensor_copy(w_int[:, 1], q_nibble))
            then(nc.vector.reciprocal(y[:], scale_bc[:]))
            then(nc.vector.tensor_tensor(zero_bc[:], zero_bc[:], y[:], ALU.mult))
            then(nc.vector.tensor_scalar(zero_bc[:], zero_bc[:], ROUND, ROUND, ALU.add, ALU.subtract))
            then(nc.vector.tensor_tensor(zero_bc[:], zero_bc[:], scale_bc[:], ALU.mult))

            def iteration(i, s, do_n, do_a, do_c, do_f):
                n, a, c, f = i + 1, i, i - 1, i - 2

                def max_k(j):
                    dve.wait_ge(k_ready, 8 * a + 2 * j + 2)
                    if begun(4 * (a - 1) + j + 1):
                        dve.wait_ge(kexp_done, 4 * (a - 1) + j + 1)
                    nc.vector.tensor_reduce(k_nmax[:, j:j + 1], ps_k[:], op=ALU.max, axis=AX_X,
                                            negate=True).then_inc(kmax_done, 1)

                def shift_q(j):
                    r = j % QR
                    heads = ps_q[:].rearrange("p (h d) -> p h d", h=HEADS)
                    dve.wait_ge(q_ready, 8 * a + j + 1)
                    nc.vector.tensor_reduce(q_nmax[:, r, :], heads, op=ALU.max, axis=AX_X,
                                            negate=True).then_inc(qmax_done, 1)
                    dve.wait_ge(qmax_done, 8 * a + j + 1)
                    if begun(8 * a + j + 1 - QR):
                        dve.wait_ge(tq_ready, 8 * a + j + 1 - QR)
                    nc.vector.tensor_tensor(q_exp[:, r, :].rearrange("p (h d) -> p h d", h=HEADS), heads,
                                            q_nmax[:, r, :].unsqueeze(2).to_broadcast([P, HEADS, DH]),
                                            ALU.add).then_inc(qsub_done, 1)

                def sum_q(j):
                    r = j % QR
                    dve.wait_ge(qexp_done, 8 * a + j + 1)
                    nc.vector.tensor_reduce(q_sum[:, r, :], q_exp[:, r, :].rearrange("p (h d) -> p h d", h=HEADS),
                                            op=ALU.add, axis=AX_X).then_inc(qsum_done, 1)
                    dve.wait_ge(qsum_done, 8 * a + j + 1)
                    if begun(8 * a + j + 1 - QR):
                        dve.wait_ge(qs_done, 8 * a + j + 1 - QR)
                    nc.vector.reciprocal(q_rec[:, r, :], q_sum[:, r, :]).then_inc(qrec_done, 1)

                for j in range(STEPS):
                    if j == 0 and do_f:
                        dve.wait_ge(n2_ready, f + 1)
                        if begun(f):
                            dve.wait_ge(rn_done, f)
                        nc.vector.tensor_scalar(n2[:], ps_tk[:, 0:TC], NORM_FLOOR_SQ, None,
                                                ALU.max).then_inc(n2_moved, 1)
                    if j < HC and do_a:
                        max_k(j)
                    if do_a:
                        shift_q(j)
                    if j == 2 and do_f:
                        dve.wait_ge(x2_done, f + 1)
                        if begun(4 * f):
                            dve.wait_ge(rstd2_steps, 4 * f)
                        for h in range(HALVES):
                            nc.vector.bn_stats(stats2[:, h, :], halves(x2)[h]).then_inc(stats2_part, 1)
                        dve.wait_ge(stats2_part, 2 * (f + 1))
                    if j == 3 and do_n:
                        dve.wait_ge(x_loaded[1 - s], loads(n, 1 - s))
                        if begun(n):
                            dve.wait_ge(ve1_done, n)
                        if begun(n):
                            dve.wait_ge(xn_done, n)
                        for h in range(HALVES):
                            nc.vector.bn_stats(stats1[:, h, :], halves(x_in[1 - s])[h]).then_inc(stats1_part, 1)
                        dve.wait_ge(stats1_part, 2 * (n + 1))
                    if j >= 1 and do_a:
                        sum_q(j - 1)
                    if j == 2 and do_f:
                        nc.vector.bn_aggr(mv2[:], stats2[:].rearrange("p a b -> p (a b)")).then_inc(stats2_done, 1)
                    if j == 3 and do_n:
                        nc.vector.bn_aggr(mv1[:], stats1[:].rearrange("p a b -> p (a b)")).then_inc(stats1_done, 1)
                    if j == 1 and do_f:
                        for h in range(HALVES):
                            dve.wait_ge(rb_ready, 2 * f + h + 1)
                            dve.wait_ge(og_done, 2 * f + h + 1)
                            if begun(f):
                                dve.wait_ge(x2_done, f)
                            nc.vector.tensor_tensor(halves(att)[h], halves(og)[h], ps_o[h][:],
                                                    ALU.mult).then_inc(att_done, 1)
                    if j == 3 and do_c:
                        dve.wait_ge(kexp_done, 4 * (c + 1))
                        nc.vector.reciprocal(k_rec[:], k_sum[:, 1 - s, :]).then_inc(krec_done, 1)
                        dve.wait_ge(krec_done, 2 * c + 1)
                        nc.vector.tensor_scalar(k_rec[:], k_rec[:], q_scale, None, ALU.mult).then_inc(krec_done, 1)
                        dve.wait_ge(krec_done, 2 * c + 2)
                        dve.wait_ge(g_ready, c + 1)
                        nc.vector.tensor_tensor(g_t[:], ps_m[:].rearrange("p (c o) -> p c o", c=HC),
                                                k_rec[:].unsqueeze(2).to_broadcast([P, HC, P]),
                                                ALU.mult).then_inc(g_moved, 1)
                    if j == 4 and do_f:
                        for h in range(2):
                            dve.wait_ge(x2hi_done, 2 * f + h + 1)
                            nc.vector.tensor_tensor(x2_lo[:, 4 * h:4 * h + 4, :],
                                                    ps_o[h][:].rearrange("p (t c) -> p t c", t=4),
                                                    x2_hi[:, 4 * h:4 * h + 4, :],
                                                    ALU.subtract).then_inc(x2lo_done, 1)
                    if j == 5 and do_f:
                        dve.wait_ge(x2n_done, f + 1)
                        nc.vector.tensor_scalar(nrs2[:], rs2[:], -1.0, None, ALU.mult).then_inc(nrs_done, 1)
                        dve.wait_ge(nrs_done, f + 1)
                        dve.wait_ge(x2b_done, f + 1)
                        nc.vector.scalar_tensor_tensor(out=x2b[:], in0=zero_bc[:], scalar=nrs2[:], in1=x2b[:],
                                                       op0=ALU.mult, op1=ALU.add).then_inc(x2c_done, 1)
                    if j == 5 and do_n:
                        dve.wait_ge(rstd1_done, n + 1)
                        if begun(n):
                            dve.wait_ge(xnlo_done, n)
                        nc.vector.tensor_scalar(xn[:], x_in[1 - s][:], mv1[:, 0:1], rstd1[:], ALU.subtract,
                                                ALU.mult).then_inc(xn_done, 1)
                    if j >= 6 and do_f:
                        h = j - 6
                        dve.wait_ge(y_ready, 2 * f + h + 1)
                        if h == 0:
                            if begun(16 * f):
                                dve.wait_ge(y_stored, 16 * f)
                        nc.vector.tensor_tensor(halves(y)[h], ps_m[:], halves(scale_bc)[h],
                                                ALU.mult).then_inc(ymul_done, 1)
                        dve.wait_ge(ymul_done, 2 * f + h + 1)
                        dve.wait_ge(x2c_done, f + 1)
                        nc.vector.tensor_tensor(halves(y)[h], halves(y)[h], halves(x2b)[h],
                                                ALU.add).then_inc(y_done, 1)
                if do_a:
                    sum_q(STEPS - 1)

            pipeline(dve, iteration)

        @block.tensor
        def _(pe):
            pe.wait_ge(w_loaded, 160)
            pe.wait_ge(consts_made, 6)
            for w, ps in ((wq_in, ps_q), (wk_in, ps_tq)):
                for c in range(HC):
                    nc.tensor.transpose(ps[:, c * P:(c + 1) * P], w[:, c, :], ident[:])
            for c in range(HC):
                last = nc.tensor.transpose(ps_tk[:, c * P:(c + 1) * P], wo_in[:, c * P:(c + 1) * P], ident[:])
            last.then_inc(set_pe, 1)
            pe.wait_ge(set_dve, 7)
            for h in range(HEADS):
                rows = slice(DH * (h % 2), DH * (h % 2) + DH)
                at = (h % 2) * BANK + (h // 2) * P
                last = nc.tensor.matmul(ps_k[:, at:at + P], wv_in[rows, h // 2, :], wo_t[rows, h // 2, :],
                                        start=True, stop=True)
            last.then_inc(set_pe, 1)
            pe.wait_ge(set_dve, 17)

            def iteration(i, s, do_n, do_a, do_c, do_f):
                n, a, c, f = i + 1, i, i - 1, i - 2

                def three(ps, lhs_hi, lhs_lo, rhs_hi, rhs_lo):
                    nc.tensor.matmul(ps, lhs_lo, rhs_hi, start=True, stop=False)
                    nc.tensor.matmul(ps, lhs_hi, rhs_lo, start=False, stop=False)
                    return nc.tensor.matmul(ps, lhs_hi, rhs_hi, start=False, stop=True)

                def project_k(j):
                    fc = slice(j * P, (j + 1) * P)
                    if j == 0:
                        pe.wait_ge(chi_done, a + 1)
                        pe.wait_ge(clo_done, a + 1)
                    if begun(4 * a + j):
                        pe.wait_ge(kexp_done, 4 * a + j)
                    for h in range(HALVES):
                        three(halves(ps_k)[h], wk_hi[:, fc], wk_lo[:, fc], halves(c_hi)[h],
                              halves(c_lo)[h]).then_inc(k_ready, 1)

                def project_q(j):
                    tc = slice(j * P, (j + 1) * P)
                    if j == 0:
                        pe.wait_ge(xnhi_done, a + 1)
                        pe.wait_ge(xnlo_done, a + 1)
                    if begun(8 * a + j):
                        pe.wait_ge(qsub_done, 8 * a + j)
                    three(ps_q[:], xn_hi[s][:, tc], xn_lo[s][:, tc], wq_hi[:], wq_lo[:]).then_inc(q_ready, 1)

                def transpose_q(b, j):
                    pe.wait_ge(qs_done, 8 * b + j + 1)
                    if begun(8 * b + j):
                        pe.wait_ge(tq_moved, 8 * b + j)
                    for fc in range(HC):
                        last = nc.tensor.transpose(ps_tq[:, fc * P:(fc + 1) * P],
                                                   q_exp[:, j % QR, fc * P:(fc + 1) * P], ident[:])
                    last.then_inc(tq_ready, 1)

                def transpose_k(k):
                    pe.wait_ge(kexp_done, 4 * a + k // 2 + 1)
                    if begun(8 * a + k):
                        pe.wait_ge(tk_moved, 8 * a + k)
                    for t in range(4):
                        tok = (4 * (k % 2) + t) * P
                        last = nc.tensor.transpose(ps_tk[:, t * P:(t + 1) * P],
                                                   k_exp[:, (k // 2) % 2, tok:tok + P], ident[:])
                    last.then_inc(tk_ready, 1)

                def mix_m(t0, t1):
                    if t0 == 0:
                        pe.wait_ge(tk_moved, 8 * (c + 1))
                        pe.wait_ge(tc_moved, 2 * (c + 1))
                        if begun(2 * (c - 1)):
                            pe.wait_ge(ymul_done, 2 * (c - 1))
                    for t in range(t0, t1):
                        last = nc.tensor.matmul(ps_m[:], c_t[1 - s][:, t, :], k_t[:, t, :], start=(t == 0),
                                                stop=(t == TC - 1))
                    if t1 == TC:
                        last.then_inc(m_ready, 1)

                def mix_g():
                    pe.wait_ge(m_moved, c + 1)
                    for h in range(HEADS):
                        rows = slice(DH * (h % 2), DH * (h % 2) + DH)
                        last = nc.tensor.matmul(ps_m[rows, (h // 2) * P:(h // 2 + 1) * P],
                                                m_t[:, h * DH:(h + 1) * DH], vo[:, h * P:(h + 1) * P],
                                                start=True, stop=True)
                    last.then_inc(g_ready, 1)

                def mix_out(k0, k1):
                    for k in range(k0, k1):
                        h, fc = k // HC, k % HC
                        if k == 0:
                            pe.wait_ge(g_moved, c + 1)
                            pe.wait_ge(tq_moved, 8 * (c + 1))
                        if fc == 0:
                            if do_a:
                                pe.wait_ge(tc_moved, 2 * a + h + 1)
                            if do_f:
                                pe.wait_ge(x2lo_done, 2 * f + h + 1)
                        last = nc.tensor.matmul(ps_o[h][:], g_t[:, fc, :], halves_q(h)[:, fc, :], start=(fc == 0),
                                                stop=(fc == HC - 1))
                        if fc == HC - 1:
                            last.then_inc(out_ready, 1)

                def halves_q(h):
                    return q_t[1 - s][:, :, h * BANK:(h + 1) * BANK]

                def feed_forward(h, k0, k1):
                    for k in range(k0, k1):
                        if k == 0:
                            if h == 0:
                                pe.wait_ge(x2hi_done, 2 * (f + 1))
                                pe.wait_ge(x2lo_done, 2 * (f + 1))
                                if do_c:
                                    pe.wait_ge(g_moved, c + 1)
                            else:
                                pe.wait_ge(ymul_done, 2 * f + 1)
                        w = halves(w_int[:, k // RC, k % RC, :])[h]
                        nc.tensor.matmul(ps_m[:], x2_lo[:, k, :], w, start=(k == 0), stop=False)
                        last = nc.tensor.matmul(ps_m[:], x2_hi[:, k, :], w, start=False, stop=(k == TC - 1))
                    if k1 == TC:
                        last.then_inc(y_ready, 1)

                for j in range(STEPS):
                    if j == 0 and do_f:
                        pe.wait_ge(sq_done, 2 * (f + 1))
                        if do_c:
                            pe.wait_ge(tk_moved, 8 * (c + 1))
                        for t in range(TC):
                            last = nc.tensor.matmul(ps_tk[:, t:t + 1], sq[:, t * P:(t + 1) * P], ones[:],
                                                    start=True, stop=True)
                        last.then_inc(n2_ready, 1)
                    if 2 <= j < 6 and do_a:
                        if j == 2 and do_f:
                            pe.wait_ge(n2_moved, f + 1)
                        transpose_k(2 * (j - 2))
                    if j < HC and do_a:
                        project_k(j)
                    if 2 <= j < 6 and do_a:
                        transpose_k(2 * (j - 2) + 1)
                    if do_a:
                        project_q(j)
                    if j < 2 and do_c:
                        transpose_q(c, 6 + j)
                    if j >= 2 and do_a:
                        transpose_q(a, j - 2)
                    if j < 2 and do_c:
                        mix_m(4 * j, 4 * j + 4)
                    if j == 1 and do_f:
                        pe.wait_ge(rn_done, f + 1)
                        pe.wait_ge(og_done, 2 * (f + 1))
                        for t in range(TC):
                            last = nc.tensor.transpose(ps_o[t // 4][:, (t % 4) * P:(t % 4 + 1) * P],
                                                       rn[:, t:t + 1].to_broadcast([P, P]), ident[:])
                            if t % 4 == 3:
                                last.then_inc(rb_ready, 1)
                    if j == 2 and do_a:
                        for h in range(2):
                            if do_f:
                                pe.wait_ge(att_done, 2 * f + h + 1)
                            for t in range(4):
                                tok = (4 * h + t) * P
                                last = nc.tensor.transpose(ps_o[h][:, t * P:(t + 1) * P],
                                                           c_in[s][:, tok:tok + P], ident[:])
                            last.then_inc(tc_ready, 1)
                    if j == 3 and do_c:
                        mix_g()
                    if j == 4 and do_f:
                        pe.wait_ge(x2n_done, f + 1)
                        for h in range(2):
                            if do_a:
                                pe.wait_ge(tc_moved, 2 * a + h + 1)
                            for m in range(RC):
                                last = nc.tensor.transpose(ps_o[h][:, m * P:(m + 1) * P],
                                                           x2n[:, h, m * P:(m + 1) * P], ident[:])
                            last.then_inc(tx_ready, 1)
                    if j >= 5:
                        if do_f:
                            if j == 5:
                                feed_forward(0, 0, TC)
                            if j == 6:
                                feed_forward(1, 0, TC // 2)
                            if j == 7:
                                feed_forward(1, TC // 2, TC)
                        if do_c:
                            mix_out(3 * (j - 5), min(3 * (j - 5) + 3, 2 * HC))

            pipeline(pe, iteration)


_INS = ["x", "ctx_4096", "L0_xattn_Wq", "L0_xattn_Wk", "L0_xattn_Wv", "L0_xattn_Wo", "L0_xattn_bo", "L0_xattn_g",
        "L0_ffn_qweight", "L0_ffn_scales", "L0_ffn_zeros", "L0_ffn_bias"]


def kernel(**inputs):
    import concourse.bacc as bacc
    from concourse.bass_utils import run_bass_kernel_spmd

    nc = bacc.Bacc("TRN2", target_bir_lowering=False, num_devices=1)
    arrays, args = {}, []
    for name in _INS:
        a = np.ascontiguousarray(inputs[name])
        arrays[f"in_{name}"] = a
        args.append(nc.dram_tensor(f"in_{name}", a.shape, mybir.dt.from_np(a.dtype), kind="ExternalInput").ap())
    out = nc.dram_tensor("out_x", inputs["x"].shape, F32, kind="ExternalOutput").ap()
    build(nc, *args, out)
    r = run_bass_kernel_spmd(nc, [arrays], core_ids=[0])
    return r.results[0]["out_x"]
```

```python
from contextlib import ExitStack

import numpy as np

import concourse.bass as bass
from concourse import mybir

F32 = mybir.dt.float32
F32R = mybir.dt.float32r
F16 = mybir.dt.float16
I32 = mybir.dt.int32
ALU = mybir.AluOpType
ACT = mybir.ActivationFunctionType
AX_X = mybir.AxisListType.X

P = 128
BANK = 512
STEPS = 8
LN_EPS = 1e-5
NORM_FLOOR_SQ = 1e-24
ROUND = 1.5 * 2.0 ** 23


def build(nc, x, ctx_in, wq, wk, wv, wo, bo, g, qweight, scales, zeros, bias, out):
    NB, DIM, N = x.shape
    HID = wq.shape[0]
    DH = 64
    HEADS = HID // DH
    HC = HID // P
    TC = N // P
    HALVES = N // BANK
    OUT = qweight.shape[1]
    RC = qweight.shape[0] // P
    assert DIM == P and TC == STEPS and HC == 4 and OUT == N and 2 * RC == TC
    q_scale = DH ** -0.5
    g_scale = float(np.sqrt(DIM))

    with ExitStack() as ctx:
        def sb(name, shape, dt=F32):
            return ctx.enter_context(nc.sbuf_tensor(name, shape, dt))

        def psum(name, shape):
            return ctx.enter_context(nc.psum_tensor(name, shape, F32))

        def sem(name):
            return ctx.enter_context(nc.semaphore(name))

        ident = sb("ident", [P, P])
        ones = sb("ones", [P, 1])
        neg_half = sb("neg_half", [P, TC])
        eps_col = sb("eps_col", [P, 1])
        minus_col = sb("minus_col", [P, 1])
        wq_hi = sb("wq_hi", [P, HID], F32R)
        wq_lo = sb("wq_lo", [P, HID], F32R)
        wk_hi = sb("wk_hi", [P, HID], F32R)
        wk_lo = sb("wk_lo", [P, HID], F32R)
        vo = sb("vo", [P, HEADS * P])
        w_int = sb("w_int", [P, 2, RC, OUT], F16)
        scale_bc = sb("scale_bc", [P, OUT])
        zero_bc = sb("zero_bc", [P, OUT])
        bias_bc = sb("bias_bc", [P, OUT])
        bo_col = sb("bo_col", [P, 1])
        gs_col = sb("gs_col", [P, 1])
        bogs_col = sb("bogs_col", [P, 1])

        x_in = [sb(f"x_in{s}", [P, N]) for s in range(2)]
        c_in = [sb(f"c_in{s}", [P, N]) for s in range(2)]
        x_res = sb("x_res", [P, N])
        xn = sb("xn", [P, N])
        xn_hi = [sb(f"xn_hi{s}", [P, N], F32R) for s in range(2)]
        xn_lo = [sb(f"xn_lo{s}", [P, N], F32R) for s in range(2)]
        c_hi = sb("c_hi", [P, N], F32R)
        c_lo = sb("c_lo", [P, N], F32R)
        c_t = sb("c_t", [P, TC, P])
        stats1 = sb("stats1", [P, 2, 6])
        mv1 = sb("mv1", [P, 2])
        ve1 = sb("ve1", [P, 1])
        rstd1 = sb("rstd1", [P, 1])
        QR = 8
        q_exp = sb("q_exp", [P, QR, HID])
        q_nmax = sb("q_nmax", [P, QR, HEADS])
        q_sum = sb("q_sum", [P, QR, HEADS])
        q_rec = sb("q_rec", [P, QR, HEADS])
        k_exp = sb("k_exp", [P, 2, N])
        k_nmax = sb("k_nmax", [P, HC])
        k_sum = sb("k_sum", [P, 2, HC])
        k_rec = sb("k_rec", [P, HC])
        k_t = sb("k_t", [P, TC, HID])
        q_hi = sb("q_hi", [P, HC, N], F32R)
        q_lo = sb("q_lo", [P, HC, N], F32R)
        m_t = sb("m_t", [P, HID])
        g_t = sb("g_t", [P, HC, P])
        g_hi = sb("g_hi", [P, HC, P], F32R)
        g_lo = sb("g_lo", [P, HC, P], F32R)
        og = sb("og", [P, N])
        sq = sb("sq", [P, N])
        n2 = sb("n2", [P, TC])
        rn = sb("rn", [P, TC])
        x2 = sb("x2", [P, N])
        stats2 = sb("stats2", [P, 2, 6])
        mv2 = sb("mv2", [P, 2])
        ve2 = sb("ve2", [P, 1])
        rstd2 = sb("rstd2", [P, 1])
        nm2 = sb("nm2", [P, 1])
        nmr2 = sb("nmr2", [P, 1])
        rs2 = sb("rs2", [P, 1])
        nrs2 = sb("nrs2", [P, 1])
        x2n = og[:].rearrange("p (t r) -> p t r", t=2)
        x2b = sb("x2b", [P, N])
        x2_hi = sb("x2_hi", [P, TC, P], F16)
        x2_lo = sb("x2_lo", [P, TC, P], F16)
        y = sb("y", [P, OUT])

        q_packed = [t[:].bitcast(I32) for t in (og, sq, x2b, x2)]
        q_nibble = y[:].bitcast(I32)
        k_flat = k_t[:].rearrange("p t h -> p (t h)")
        wq_in = k_flat[:, 0:HID].rearrange("p (k c) -> p k c", k=HC)
        wk_in = k_flat[:, HID:2 * HID].rearrange("p (k c) -> p k c", k=HC)
        wv_in = k_flat[:, 2 * HID:3 * HID].rearrange("p (k c) -> p k c", k=HC)
        wo_in = k_flat[:, 3 * HID:4 * HID]
        wo_t = k_flat[:, 4 * HID:5 * HID].rearrange("p (k o) -> p k o", k=HC)
        wq_tf = k_flat[:, 5 * HID:6 * HID]
        wk_tf = k_flat[:, 6 * HID:7 * HID]

        ps_q = psum("ps_q", [P, BANK])
        ps_k = psum("ps_k", [P, HALVES * BANK])
        ps_ta = psum("ps_ta", [P, BANK])
        ps_tb = psum("ps_tb", [P, BANK])
        ps_m = psum("ps_m", [P, BANK])
        ps_o = [psum(f"ps_o{h}", [P, BANK]) for h in range(2)]

        w_loaded = sem("w_loaded")
        rows_loaded = sem("rows_loaded")
        qw_loaded = sem("qw_loaded")
        consts_made = sem("consts_made")
        gs_done = sem("gs_done")
        set_dve = sem("set_dve")
        set_pe = sem("set_pe")
        unpack_steps = sem("unpack_steps")
        x_loaded = [sem(f"x_loaded{s}") for s in range(2)]
        c_loaded = [sem(f"c_loaded{s}") for s in range(2)]
        xres_loaded = sem("xres_loaded")
        y_stored = sem("y_stored")
        stats1_part = sem("stats1_part")
        stats1_done = sem("stats1_done")
        ve1_done = sem("ve1_done")
        rstd1_done = sem("rstd1_done")
        xn_done = sem("xn_done")
        xnhi_done = sem("xnhi_done")
        xnlo_done = sem("xnlo_done")
        chi_done = sem("chi_done")
        clo_done = sem("clo_done")
        q_ready = sem("q_ready")
        k_ready = sem("k_ready")
        qmax_done = sem("qmax_done")
        qsub_done = sem("qsub_done")
        qexp_done = sem("qexp_done")
        qsum_done = sem("qsum_done")
        qrec_done = sem("qrec_done")
        qs_done = sem("qs_done")
        tq_ready = sem("tq_ready")
        tq_moved = sem("tq_moved")
        qlo_done = sem("qlo_done")
        kmax_done = sem("kmax_done")
        kexp_done = sem("kexp_done")
        tk_ready = sem("tk_ready")
        tk_moved = sem("tk_moved")
        tc_ready = sem("tc_ready")
        tc_moved = sem("tc_moved")
        m_ready = sem("m_ready")
        m_moved = sem("m_moved")
        krec_done = sem("krec_done")
        g_ready = sem("g_ready")
        g_moved = sem("g_moved")
        g_split = sem("g_split")
        out_ready = sem("out_ready")
        og_done = sem("og_done")
        sq_done = sem("sq_done")
        n2_ready = sem("n2_ready")
        n2_moved = sem("n2_moved")
        rn_done = sem("rn_done")
        rb_ready = sem("rb_ready")
        att_done = sem("att_done")
        x2_done = sem("x2_done")
        stats2_part = sem("stats2_part")
        stats2_done = sem("stats2_done")
        rstd2_steps = sem("rstd2_steps")
        x2n_done = sem("x2n_done")
        nrs_done = sem("nrs_done")
        x2b_done = sem("x2b_done")
        x2c_done = sem("x2c_done")
        tx_ready = sem("tx_ready")
        x2hi_done = sem("x2hi_done")
        x2lo_done = sem("x2lo_done")
        y_ready = sem("y_ready")
        ymul_done = sem("ymul_done")
        y_done = sem("y_done")

        def begun(value):
            return not isinstance(value, int) or value > 0

        def loads(b, s):
            return 8 * (b - s) + 16

        FIRST, LAST = -1, NB + 2
        LOOP = (3, NB - 1)

        def pipeline(eng, iteration, end=LOOP[1]):
            def peeled(i):
                iteration(i, i % 2, i + 1 < NB, 0 <= i < NB, 0 <= i - 1 < NB, 0 <= i - 2 < NB)

            for i in range(FIRST, LOOP[0]):
                peeled(i)
            with eng.Fori(LOOP[0], end, 2) as i:
                iteration(i, LOOP[0] % 2, True, True, True, True)
                iteration(i + 1, (LOOP[0] + 1) % 2, True, True, True, True)
            for i in range(end, LAST):
                peeled(i)

        def halves(ap):
            return [ap[:, h * BANK:(h + 1) * BANK] for h in range(HALVES)]

        block = ctx.enter_context(nc.Block())

        @block.sync
        def _(sp):
            def load_x(b, s):
                sp.dma_start(x_in[s][:], x[b]).then_inc(x_loaded[s], 16)

            def load_c(b, s):
                sp.dma_start(c_in[s][:], ctx_in[b]).then_inc(c_loaded[s], 16)

            load_x(0, 0)
            for dst, src in (
                (wq_in, wq.rearrange("(k p) c -> p k c", p=P)),
                (wk_in, wk.rearrange("(k p) c -> p k c", p=P)),
                (wo_in, wo),
                (wv_in, wv.rearrange("(k p) c -> p k c", p=P)),
                (bo_col[:], bo.rearrange("(p a) -> p a", a=1)),
                (gs_col[:], g.rearrange("a p b -> (a p) b")),
            ):
                sp.dma_start(dst, src).then_inc(w_loaded, 16)
            load_c(0, 0)
            for m in range(RC):
                sp.dma_start(q_packed[m], qweight[m * P:(m + 1) * P, :]).then_inc(qw_loaded, 16)
            load_x(1, 1)
            load_c(1, 1)
            for dst, src in (
                (scale_bc[:], scales.rearrange("n a -> a n").to_broadcast([P, OUT])),
                (zero_bc[:], zeros.rearrange("n a -> a n").to_broadcast([P, OUT])),
                (bias_bc[:], bias.rearrange("(a n) -> a n", a=1).to_broadcast([P, OUT])),
            ):
                sp.dma_start(dst, src).then_inc(rows_loaded, 16)

            def kept(value):
                return value if isinstance(value, int) else sp.snap(value)

            def iteration(i, s, do_n, do_a, do_c, do_f):
                c, f = i - 1, i - 2
                if do_c:
                    before = kept(2 * c)
                    sp.wait_ge(w_loaded, 96)
                    if begun(c):
                        sp.wait_ge(x2_done, before)
                    sp.dma_start(x_res[:], x[c]).then_inc(xres_loaded, 16)
                if not isinstance(i, int) or 0 <= i < NB - 2:
                    after, twice = kept(i + 1), kept(2 * (i + 1))
                    sp.wait_ge(w_loaded, 96)
                    sp.wait_ge(xn_done, after)
                    sp.dma_start(x_in[s][:], x[i + 2]).then_inc(x_loaded[s], 16)
                    sp.wait_ge(w_loaded, 96)
                    sp.wait_ge(chi_done, after)
                    sp.wait_ge(clo_done, after)
                    sp.wait_ge(tc_ready, twice)
                    sp.dma_start(c_in[s][:], ctx_in[i + 2]).then_inc(c_loaded[s], 16)
                if do_f:
                    finished = kept(2 * (f + 1))
                    sp.wait_ge(w_loaded, 96)
                    sp.wait_ge(y_done, finished)
                    sp.dma_start(out[f], y[:]).then_inc(y_stored, 16)

            pipeline(sp, iteration, end=NB - 3)
            sp.wait_ge(y_stored, 16 * NB)

        @block.gpsimd
        def _(pool):
            nc.gpsimd.memset(ident[:], 0.0).then_inc(consts_made, 1)
            nc.gpsimd.memset(ones[:], 1.0).then_inc(consts_made, 1)
            nc.gpsimd.memset(neg_half[:], -0.5).then_inc(consts_made, 1)
            nc.gpsimd.memset(eps_col[:], LN_EPS).then_inc(consts_made, 1)
            nc.gpsimd.memset(minus_col[:], -1.0).then_inc(consts_made, 1)
            pool.wait_ge(consts_made, 5)
            nc.gpsimd.affine_select(out=ident[:], in_=ident[:], compare_op=ALU.not_equal, fill=1.0,
                                    base=0, pattern=[[-1, P]], channel_multiplier=1).then_inc(consts_made, 1)

            def iteration(i, s, do_n, do_a, do_c, do_f):
                n, a, c, f = i + 1, i, i - 1, i - 2

                def scale_q(b, j):
                    pool.wait_ge(qrec_done, 8 * b + j + 1)
                    chunk = q_exp[:, j, :].rearrange("p (h d) -> p h d", h=HEADS)
                    rec = q_rec[:, j, :].unsqueeze(2).to_broadcast([P, HEADS, DH])
                    nc.gpsimd.tensor_tensor(chunk, chunk, rec, ALU.mult).then_inc(qs_done, 1)

                def add_y(h):
                    pool.wait_ge(ymul_done, 2 * f + h + 1)
                    pool.wait_ge(x2c_done, f + 1)
                    nc.gpsimd.tensor_tensor(halves(y)[h], halves(y)[h], halves(x2b)[h], ALU.add).then_inc(y_done, 1)

                for j in range(STEPS):
                    if j == 7 and do_c:
                        for h in range(HALVES):
                            pool.wait_ge(att_done, 2 * c + h + 1)
                            if h == 0:
                                pool.wait_ge(xres_loaded, 16 * (c + 1))
                                if begun(c):
                                    pool.wait_ge(x2n_done, c)
                            nc.gpsimd.tensor_tensor(halves(x2)[h], halves(og)[h], halves(x_res)[h],
                                                    ALU.add).then_inc(x2_done, 1)
                    if j == 0 and do_c:
                        scale_q(c, STEPS - 1)
                    if j == 0 and do_f:
                        pool.wait_ge(stats2_done, f + 1)
                        nc.gpsimd.tensor_tensor(ve2[:], mv2[:, 1:2], eps_col[:], ALU.add).then_inc(rstd2_steps, 1)
                        nc.gpsimd.tensor_tensor(nm2[:], mv2[:, 0:1], minus_col[:], ALU.mult).then_inc(rstd2_steps, 1)
                        pool.wait_ge(rstd2_steps, 4 * f + 1)
                        nc.gpsimd.tensor_tensor(rstd2[:], ve2[:], neg_half[:, 0:1], ALU.pow).then_inc(rstd2_steps, 1)
                        pool.wait_ge(rstd2_steps, 4 * f + 3)
                        nc.gpsimd.tensor_tensor(nmr2[:], nm2[:], rstd2[:], ALU.mult).then_inc(rstd2_steps, 1)
                    if j >= 1 and do_a:
                        scale_q(a, j - 1)
                    if j in (6, 7) and do_f:
                        add_y(j - 6)
                    if j == 1 and do_f:
                        if isinstance(i, int) and i == 2:
                            pool.wait_ge(rows_loaded, 48)
                        if begun(2 * f):
                            pool.wait_ge(y_done, 2 * f)
                        pool.wait_ge(x2_done, 2 * (f + 1))
                        nc.gpsimd.tensor_tensor(x2b[:], x2[:], bias_bc[:], ALU.add).then_inc(x2b_done, 1)
                    if j == 4 and do_n:
                        pool.wait_ge(stats1_done, n + 1)
                        nc.gpsimd.tensor_tensor(ve1[:], mv1[:, 1:2], eps_col[:], ALU.add).then_inc(ve1_done, 1)
                        pool.wait_ge(ve1_done, n + 1)
                        nc.gpsimd.tensor_tensor(rstd1[:], ve1[:], neg_half[:, 0:1], ALU.pow).then_inc(rstd1_done, 1)
                    if j == 4 and do_n:
                        pool.wait_ge(chi_done, n + 1)
                        nc.gpsimd.tensor_tensor(c_lo[:], c_in[1 - s][:], c_hi[:].bitcast(F32),
                                                ALU.subtract).then_inc(clo_done, 1)
                    if j == 6 and do_n:
                        pool.wait_ge(xnhi_done, n + 1)
                        if begun(8 * a):
                            pool.wait_ge(q_ready, 8 * a)
                        nc.gpsimd.tensor_tensor(xn_lo[1 - s][:], xn[:], xn_hi[1 - s][:].bitcast(F32),
                                                ALU.subtract).then_inc(xnlo_done, 1)
                    if j == 5 and do_c:
                        pool.wait_ge(n2_moved, c + 1)
                        nc.gpsimd.tensor_tensor(rn[:], n2[:], neg_half[:], ALU.pow).then_inc(rn_done, 1)

            pipeline(pool, iteration)

        @block.scalar
        def _(act):
            act.wait_ge(w_loaded, 96)
            nc.scalar.mul(gs_col[:], gs_col[:], g_scale).then_inc(gs_done, 1)

            def iteration(i, s, do_n, do_a, do_c, do_f):
                n, a, c, f = i + 1, i, i - 1, i - 2

                def exp_k(j):
                    act.wait_ge(kmax_done, 4 * a + j + 1)
                    if begun(8 * a + 2 * (j - 2) + 2):
                        act.wait_ge(tk_ready, 8 * a + 2 * (j - 2) + 2)
                    nc.scalar.activation(k_exp[:, j % 2, :], ps_k[:], ACT.Exp, bias=k_nmax[:, j:j + 1],
                                         accum_out=k_sum[:, s, j:j + 1]).then_inc(kexp_done, 1)

                def exp_q(j):
                    act.wait_ge(qsub_done, 8 * a + j + 1)
                    nc.scalar.activation(q_exp[:, j, :], q_exp[:, j, :], ACT.Exp).then_inc(qexp_done, 1)

                def move_tq(b, j):
                    act.wait_ge(tq_ready, 8 * b + j + 1)
                    if begun(2 * (b - 1) + j // 4 + 1):
                        act.wait_ge(out_ready, 2 * (b - 1) + j // 4 + 1)
                    nc.scalar.activation(q_hi[:, :, j * P:(j + 1) * P],
                                         ps_tb[:].rearrange("p (c t) -> p c t", c=HC),
                                         ACT.Copy).then_inc(tq_moved, 1)

                def move_tk(k):
                    t0, fc = 4 * (k % 2), k // 2
                    act.wait_ge(tk_ready, 8 * a + k + 1)
                    if k == 0 and begun(a):
                        act.wait_ge(m_ready, a)
                    nc.scalar.activation(k_t[:, t0:t0 + 4, fc * P:(fc + 1) * P],
                                         (ps_ta, ps_tb)[k % 2][:].rearrange("p (t c) -> p t c", t=4),
                                         ACT.Copy).then_inc(tk_moved, 1)

                def squares(h):
                    act.wait_ge(out_ready, 2 * c + h + 1)
                    if h == 0 and begun(c):
                        act.wait_ge(n2_ready, c)
                    nc.scalar.activation(halves(sq)[h], ps_o[h][:], ACT.Square, bias=bo_col[:]).then_inc(sq_done, 1)
                    if do_f and h == 0:
                        act.wait_ge(tx_ready, 2 * (f + 1))
                    nc.scalar.activation(halves(og)[h], ps_o[h][:], ACT.Identity, bias=bogs_col[:],
                                         scale=gs_col[:]).then_inc(og_done, 1)

                for j in range(STEPS):
                    if j <= 4 and do_c:
                        move_tq(c, j + 3)
                    if j >= 5 and do_a:
                        move_tq(a, j - 5)
                    if j == 5 and do_c:
                        squares(1)
                    if 2 <= j < 6 and do_a:
                        move_tk(2 * (j - 2))
                        move_tk(2 * (j - 2) + 1)
                    if j == 1 and do_f:
                        act.wait_ge(rstd2_steps, 4 * (f + 1))
                        if begun(f):
                            act.wait_ge(nrs_done, f)
                        nc.scalar.activation(x2n, x2[:].rearrange("p (r t) -> p t r", t=2), ACT.Identity,
                                             bias=nmr2[:], scale=rstd2[:], accum_out=rs2[:]).then_inc(x2n_done, 1)
                    if j < HC and do_a:
                        exp_k(j)
                    if do_a:
                        exp_q(j)
                    if j == 1 and do_f:
                        for h in range(2):
                            act.wait_ge(tx_ready, 2 * f + h + 1)
                            if h == 0 and begun(2 * f):
                                act.wait_ge(y_ready, 2 * f)
                            nc.scalar.activation(x2_hi[:, 4 * h:4 * h + 4, :],
                                                 ps_o[h][:].rearrange("p (t c) -> p t c", t=4),
                                                 ACT.Copy).then_inc(x2hi_done, 1)
                    if j == 1 and do_c:
                        act.wait_ge(m_ready, c + 1)
                        if begun(c):
                            act.wait_ge(g_ready, c)
                        nc.scalar.activation(m_t[:], ps_m[:], ACT.Copy).then_inc(m_moved, 1)
                    if j == 4 and do_c:
                        squares(0)
                    if j == 4 and do_n:
                        act.wait_ge(c_loaded[1 - s], loads(n, 1 - s))
                        if begun(8 * n):
                            act.wait_ge(k_ready, 8 * n)
                        nc.scalar.activation(c_hi[:], c_in[1 - s][:], ACT.Copy).then_inc(chi_done, 1)
                    if j == 5 and do_n:
                        act.wait_ge(xn_done, n + 1)
                        if begun(8 * a):
                            act.wait_ge(q_ready, 8 * a)
                        nc.scalar.activation(xn_hi[1 - s][:], xn[:], ACT.Copy).then_inc(xnhi_done, 1)
                    if j == 7 and do_a:
                        for h in range(2):
                            act.wait_ge(tc_ready, 2 * a + h + 1)
                            nc.scalar.activation(c_t[:, 4 * h:4 * h + 4, :],
                                                 ps_o[h][:].rearrange("p (t c) -> p t c", t=4),
                                                 ACT.Copy).then_inc(tc_moved, 1)

            pipeline(act, iteration)

        @block.vector
        def _(dve):
            steps = [0]

            def then(ins):
                ins.then_inc(set_dve, 1)
                steps[0] += 1
                dve.wait_ge(set_dve, steps[0])

            dve.wait_ge(set_pe, 1)
            for ps, full, hi, lo in ((ps_q, wq_tf, wq_hi, wq_lo), (ps_ta, wk_tf, wk_hi, wk_lo)):
                then(nc.vector.tensor_copy(full, ps[:]))
                then(nc.vector.tensor_copy(hi[:], full))
                then(nc.vector.tensor_tensor(lo[:], full, hi[:].bitcast(F32), ALU.subtract))
            then(nc.vector.tensor_copy(wo_t, ps_tb[:].rearrange("p (k o) -> p k o", k=HC)))
            dve.wait_ge(set_pe, 2)
            then(nc.vector.tensor_copy(vo[:].rearrange("p (k q o) -> p q k o", q=2, o=P),
                                       ps_k[:].rearrange("p (q k o) -> p q k o", q=2, o=P)))
            dve.wait_ge(w_loaded, 96)
            dve.wait_ge(gs_done, 1)
            then(nc.vector.tensor_tensor(bogs_col[:], bo_col[:], gs_col[:], ALU.mult))

            def unpack(k):
                t, m = k // RC, k % RC
                if k == 0:
                    dve.wait_ge(qw_loaded, 16 * RC)
                nc.vector.tensor_scalar(q_nibble, q_packed[m], 4 * t, 15, ALU.logical_shift_right,
                                        ALU.bitwise_and).then_inc(unpack_steps, 1)
                dve.wait_ge(unpack_steps, 2 * k + 1)
                nc.vector.tensor_copy(w_int[:, t, m], q_nibble).then_inc(unpack_steps, 1)
                if k == 2 * RC - 1:
                    last = 2 * (k + 1)
                    dve.wait_ge(unpack_steps, last)
                    dve.wait_ge(rows_loaded, 48)
                    nc.vector.reciprocal(y[:], scale_bc[:]).then_inc(unpack_steps, 1)
                    dve.wait_ge(unpack_steps, last + 1)
                    nc.vector.tensor_tensor(y[:], zero_bc[:], y[:], ALU.mult).then_inc(unpack_steps, 1)
                    dve.wait_ge(unpack_steps, last + 2)
                    nc.vector.tensor_scalar(y[:], y[:], ROUND, ROUND, ALU.add, ALU.subtract).then_inc(unpack_steps, 1)
                    dve.wait_ge(unpack_steps, last + 3)
                    nc.vector.tensor_tensor(zero_bc[:], y[:], scale_bc[:], ALU.mult).then_inc(unpack_steps, 1)
                    dve.wait_ge(unpack_steps, last + 4)

            def iteration(i, s, do_n, do_a, do_c, do_f):
                n, a, c, f = i + 1, i, i - 1, i - 2

                def max_k(j):
                    dve.wait_ge(k_ready, 8 * a + 2 * j + 2)
                    if begun(4 * (a - 1) + j + 1):
                        dve.wait_ge(kexp_done, 4 * (a - 1) + j + 1)
                    nc.vector.tensor_reduce(k_nmax[:, j:j + 1], ps_k[:], op=ALU.max, axis=AX_X,
                                            negate=True).then_inc(kmax_done, 1)

                def shift_q(j):
                    heads = ps_q[:].rearrange("p (h d) -> p h d", h=HEADS)
                    dve.wait_ge(q_ready, 8 * a + j + 1)
                    nc.vector.tensor_reduce(q_nmax[:, j, :], heads, op=ALU.max, axis=AX_X,
                                            negate=True).then_inc(qmax_done, 1)
                    dve.wait_ge(qmax_done, 8 * a + j + 1)
                    if begun(8 * (a - 1) + j + 1):
                        dve.wait_ge(tq_ready, 8 * (a - 1) + j + 1)
                    nc.vector.tensor_tensor(q_exp[:, j, :].rearrange("p (h d) -> p h d", h=HEADS), heads,
                                            q_nmax[:, j, :].unsqueeze(2).to_broadcast([P, HEADS, DH]),
                                            ALU.add).then_inc(qsub_done, 1)

                def sum_q(b, j):
                    dve.wait_ge(qexp_done, 8 * b + j + 1)
                    nc.vector.tensor_reduce(q_sum[:, j, :], q_exp[:, j, :].rearrange("p (h d) -> p h d", h=HEADS),
                                            op=ALU.add, axis=AX_X).then_inc(qsum_done, 1)
                    dve.wait_ge(qsum_done, 8 * b + j + 1)
                    nc.vector.reciprocal(q_rec[:, j, :], q_sum[:, j, :]).then_inc(qrec_done, 1)

                def low_q(b, j):
                    dve.wait_ge(tq_moved, 8 * b + j + 1)
                    nc.vector.tensor_tensor(q_lo[:, :, j * P:(j + 1) * P],
                                            ps_tb[:].rearrange("p (c t) -> p c t", c=HC),
                                            q_hi[:, :, j * P:(j + 1) * P].bitcast(F32),
                                            ALU.subtract).then_inc(qlo_done, 1)

                def scale_y(h):
                    dve.wait_ge(y_ready, 2 * f + h + 1)
                    if h == 0 and begun(16 * f):
                        dve.wait_ge(y_stored, 16 * f)
                    nc.vector.tensor_tensor(halves(y)[h], ps_m[:], halves(scale_bc)[h],
                                            ALU.mult).then_inc(ymul_done, 1)

                for j in range(STEPS):
                    if j in (0, 1, 2, 4) and do_c:
                        low_q(c, j + 3)
                    if j >= 5 and do_a:
                        low_q(a, j - 5)
                    if j < HC and do_a:
                        max_k(j)
                    if do_a:
                        shift_q(j)
                    if j == 4 and do_n:
                        dve.wait_ge(x_loaded[1 - s], loads(n, 1 - s))
                        if begun(n):
                            dve.wait_ge(ve1_done, n)
                            dve.wait_ge(xn_done, n)
                        for h in range(HALVES):
                            nc.vector.bn_stats(stats1[:, h, :], halves(x_in[1 - s])[h]).then_inc(stats1_part, 1)
                        dve.wait_ge(stats1_part, 2 * (n + 1))
                    if j == 7 and do_f:
                        scale_y(1)
                    if j == 0 and do_f:
                        if begun(4 * f):
                            dve.wait_ge(rstd2_steps, 4 * f)
                        for h in range(HALVES):
                            dve.wait_ge(x2_done, 2 * f + h + 1)
                            nc.vector.bn_stats(stats2[:, h, :], halves(x2)[h]).then_inc(stats2_part, 1)
                        dve.wait_ge(stats2_part, 2 * (f + 1))
                    if j == 2 and do_c:
                        dve.wait_ge(krec_done, 2 * c + 2)
                        dve.wait_ge(g_ready, c + 1)
                        nc.vector.tensor_tensor(g_t[:], ps_o[0][:].rearrange("p (c o) -> p c o", c=HC),
                                                k_rec[:].unsqueeze(2).to_broadcast([P, HC, P]),
                                                ALU.mult).then_inc(g_moved, 1)
                        dve.wait_ge(g_moved, c + 1)
                        if begun(2 * c):
                            dve.wait_ge(out_ready, 2 * c)
                        nc.vector.tensor_copy(g_hi[:], g_t[:]).then_inc(g_split, 1)
                        dve.wait_ge(g_split, 2 * c + 1)
                        nc.vector.tensor_tensor(g_lo[:], g_t[:], g_hi[:].bitcast(F32),
                                                ALU.subtract).then_inc(g_split, 1)
                    if j == 2 and do_c:
                        low_q(c, 6)
                    if j == 0 and do_c:
                        sum_q(c, STEPS - 1)
                    if j >= 1 and j != 2 and do_a:
                        if j == 3:
                            sum_q(a, 1)
                        sum_q(a, j - 1)
                    if j == 4 and do_n:
                        nc.vector.bn_aggr(mv1[:], stats1[:].rearrange("p a b -> p (a b)")).then_inc(stats1_done, 1)
                    if j == 0 and do_f:
                        nc.vector.bn_aggr(mv2[:], stats2[:].rearrange("p a b -> p (a b)")).then_inc(stats2_done, 1)
                    if j == 1 and do_f:
                        for h in range(2):
                            dve.wait_ge(x2hi_done, 2 * f + h + 1)
                            nc.vector.tensor_tensor(x2_lo[:, 4 * h:4 * h + 4, :],
                                                    ps_o[h][:].rearrange("p (t c) -> p t c", t=4),
                                                    x2_hi[:, 4 * h:4 * h + 4, :],
                                                    ALU.subtract).then_inc(x2lo_done, 1)
                    if j == 5 and do_n:
                        dve.wait_ge(rstd1_done, n + 1)
                        if begun(n):
                            dve.wait_ge(xnhi_done, n)
                            dve.wait_ge(xnlo_done, n)
                        nc.vector.tensor_scalar(xn[:], x_in[1 - s][:], mv1[:, 0:1], rstd1[:], ALU.subtract,
                                                ALU.mult).then_inc(xn_done, 1)
                    if j == 4 and do_f:
                        dve.wait_ge(x2n_done, f + 1)
                        nc.vector.tensor_scalar(nrs2[:], rs2[:], -1.0, None, ALU.mult).then_inc(nrs_done, 1)
                        dve.wait_ge(nrs_done, f + 1)
                        dve.wait_ge(x2b_done, f + 1)
                        nc.vector.scalar_tensor_tensor(out=x2b[:], in0=zero_bc[:], scalar=nrs2[:], in1=x2b[:],
                                                       op0=ALU.mult, op1=ALU.add).then_inc(x2c_done, 1)
                    if j == 5 and do_c:
                        dve.wait_ge(n2_ready, c + 1)
                        if begun(c):
                            dve.wait_ge(rn_done, c)
                        nc.vector.tensor_scalar(n2[:], ps_ta[:, 0:TC], NORM_FLOOR_SQ, None,
                                                ALU.max).then_inc(n2_moved, 1)
                    if j == 5 and do_f:
                        scale_y(0)
                    if j == 6 and do_c:
                        for h in range(HALVES):
                            dve.wait_ge(rb_ready, 2 * c + h + 1)
                            dve.wait_ge(og_done, 2 * c + h + 1)
                            nc.vector.tensor_tensor(halves(og)[h], halves(og)[h], ps_o[h][:],
                                                    ALU.mult).then_inc(att_done, 1)
                    if j == 5 and do_a:
                        dve.wait_ge(kexp_done, 4 * (a + 1))
                        nc.vector.reciprocal(k_rec[:], k_sum[:, s, :]).then_inc(krec_done, 1)
                        dve.wait_ge(krec_done, 2 * a + 1)
                        nc.vector.tensor_scalar(k_rec[:], k_rec[:], q_scale, None, ALU.mult).then_inc(krec_done, 1)
                    if isinstance(i, int) and i == 0:
                        unpack(j)

            pipeline(dve, iteration)

        @block.tensor
        def _(pe):
            pe.wait_ge(consts_made, 6)
            pe.wait_ge(w_loaded, 96)
            for w, ps in ((wq_in, ps_q), (wk_in, ps_ta)):
                for k in range(HC):
                    nc.tensor.transpose(ps[:, k * P:(k + 1) * P], w[:, k, :], ident[:])
            for k in range(HC):
                last = nc.tensor.transpose(ps_tb[:, k * P:(k + 1) * P], wo_in[:, k * P:(k + 1) * P], ident[:])
            last.then_inc(set_pe, 1)
            pe.wait_ge(set_dve, 7)
            for h in range(HEADS):
                rows = slice(DH * (h % 2), DH * (h % 2) + DH)
                at = (h % 2) * BANK + (h // 2) * P
                last = nc.tensor.matmul(ps_k[:, at:at + P], wv_in[rows, h // 2, :], wo_t[rows, h // 2, :],
                                        start=True, stop=True)
            last.then_inc(set_pe, 1)
            pe.wait_ge(set_dve, 8)

            def iteration(i, s, do_n, do_a, do_c, do_f):
                n, a, c, f = i + 1, i, i - 1, i - 2

                def three(ps, lhs_hi, lhs_lo, rhs_hi, rhs_lo, start=True, stop=True):
                    nc.tensor.matmul(ps, lhs_lo, rhs_hi, start=start, stop=False)
                    nc.tensor.matmul(ps, lhs_hi, rhs_lo, start=False, stop=False)
                    return nc.tensor.matmul(ps, lhs_hi, rhs_hi, start=False, stop=stop)

                def project_k(j):
                    fc = slice(j * P, (j + 1) * P)
                    if j == 0:
                        pe.wait_ge(chi_done, a + 1)
                        pe.wait_ge(clo_done, a + 1)
                    if begun(4 * a + j):
                        pe.wait_ge(kexp_done, 4 * a + j)
                    for h in range(HALVES):
                        three(halves(ps_k)[h], wk_hi[:, fc], wk_lo[:, fc], halves(c_hi)[h],
                              halves(c_lo)[h]).then_inc(k_ready, 1)

                def project_q(j):
                    tc = slice(j * P, (j + 1) * P)
                    if j == 0:
                        pe.wait_ge(xnhi_done, a + 1)
                        pe.wait_ge(xnlo_done, a + 1)
                    if begun(8 * a + j):
                        pe.wait_ge(qsub_done, 8 * a + j)
                    three(ps_q[:], xn_hi[s][:, tc], xn_lo[s][:, tc], wq_hi[:], wq_lo[:]).then_inc(q_ready, 1)

                def transpose_q(b, j):
                    pe.wait_ge(qs_done, 8 * b + j + 1)
                    if begun(8 * b + j):
                        pe.wait_ge(qlo_done, 8 * b + j)
                    for fc in range(HC):
                        last = nc.tensor.transpose(ps_tb[:, fc * P:(fc + 1) * P],
                                                   q_exp[:, j, fc * P:(fc + 1) * P], ident[:])
                    last.then_inc(tq_ready, 1)

                def transpose_k(k, tq_before):
                    pe.wait_ge(kexp_done, 4 * a + k // 2 + 1)
                    if begun(8 * a + k - 1):
                        pe.wait_ge(tk_moved, 8 * a + k - 1)
                    if k % 2 and begun(tq_before):
                        pe.wait_ge(qlo_done, tq_before)
                    for t in range(4):
                        tok = (4 * (k % 2) + t) * P
                        last = nc.tensor.transpose((ps_ta, ps_tb)[k % 2][:, t * P:(t + 1) * P],
                                                   k_exp[:, (k // 2) % 2, tok:tok + P], ident[:])
                    last.then_inc(tk_ready, 1)

                def mix_m(t0, t1):
                    if t0 == 0:
                        pe.wait_ge(tk_moved, 8 * (c + 1))
                        pe.wait_ge(tc_moved, 2 * (c + 1))
                        if begun(2 * (c - 1)):
                            pe.wait_ge(ymul_done, 2 * (c - 1))
                    for t in range(t0, t1):
                        last = nc.tensor.matmul(ps_m[:], c_t[:, t, :], k_t[:, t, :], start=(t == 0),
                                                stop=(t == TC - 1))
                    if t1 == TC:
                        last.then_inc(m_ready, 1)

                def mix_g():
                    pe.wait_ge(m_moved, c + 1)
                    if do_f:
                        pe.wait_ge(x2lo_done, 2 * (f + 1))
                    for h in range(HEADS):
                        rows = slice(DH * (h % 2), DH * (h % 2) + DH)
                        last = nc.tensor.matmul(ps_o[0][rows, (h // 2) * P:(h // 2 + 1) * P],
                                                m_t[:, h * DH:(h + 1) * DH], vo[:, h * P:(h + 1) * P],
                                                start=True, stop=True)
                    last.then_inc(g_ready, 1)

                def mix_out(h, f0, f1):
                    tok = slice(h * BANK, (h + 1) * BANK)
                    if h == 0 and f0 == 0:
                        pe.wait_ge(g_split, 2 * (c + 1))
                    if f0 == 0:
                        pe.wait_ge(qlo_done, 8 * c + 4 * (h + 1))
                    for fc in range(f0, f1):
                        last = three(ps_o[h][:], g_hi[:, fc, :], g_lo[:, fc, :], q_hi[:, fc, tok], q_lo[:, fc, tok],
                                     start=(fc == 0), stop=(fc == HC - 1))
                    if f1 == HC:
                        last.then_inc(out_ready, 1)

                def feed_forward(h, k0, k1):
                    for k in range(k0, k1):
                        if k == 0:
                            if h == 0:
                                pe.wait_ge(x2hi_done, 2 * (f + 1))
                                pe.wait_ge(x2lo_done, 2 * (f + 1))
                                if do_c:
                                    pe.wait_ge(m_moved, c + 1)
                            else:
                                pe.wait_ge(ymul_done, 2 * f + 1)
                        w = halves(w_int[:, k // RC, k % RC, :])[h]
                        nc.tensor.matmul(ps_m[:], x2_lo[:, k, :], w, start=(k == 0), stop=False)
                        last = nc.tensor.matmul(ps_m[:], x2_hi[:, k, :], w, start=False, stop=(k == TC - 1))
                    if k1 == TC:
                        last.then_inc(y_ready, 1)

                for j in range(STEPS):
                    if 2 <= j < 6 and do_a:
                        if j == 2 and begun(a - 1):
                            pe.wait_ge(n2_moved, a - 1)
                        transpose_k(2 * (j - 2), 0)
                    if j < HC and do_a:
                        project_k(j)
                    if do_a:
                        project_q(j)
                    if j in (2, 3) and do_a:
                        transpose_k(2 * (j - 2) + 1, 8 * a + j - 4)
                    if j == 2 and do_c:
                        mix_g()
                    if j < 2 and do_c:
                        mix_m(4 * j, 4 * j + 4)
                    if j == 3 and do_c:
                        mix_out(0, 0, 2)
                    if j == 4 and do_f:
                        feed_forward(0, 0, 4)
                    if j == 5 and do_f:
                        feed_forward(0, 4, TC)
                    if j in (4, 5) and do_a:
                        transpose_k(2 * (j - 2) + 1, 8 * a + j - 4)
                    if j == 1 and do_f:
                        pe.wait_ge(x2n_done, f + 1)
                        if do_c:
                            pe.wait_ge(tc_moved, 2 * (c + 1))
                        else:
                            pe.wait_ge(att_done, 2 * (f + 1))
                        for h in range(2):
                            for m in range(RC):
                                last = nc.tensor.transpose(ps_o[h][:, m * P:(m + 1) * P],
                                                           x2n[:, h, m * P:(m + 1) * P], ident[:])
                            last.then_inc(tx_ready, 1)
                    if j == 3 and do_c:
                        mix_out(0, 2, HC)
                    if j == 4 and do_c:
                        mix_out(1, 0, HC)
                    if j == 5 and do_c:
                        pe.wait_ge(sq_done, 2 * (c + 1))
                        if do_a:
                            pe.wait_ge(tk_moved, 8 * a + 7)
                        for t in range(TC):
                            last = nc.tensor.matmul(ps_ta[:, t:t + 1], sq[:, t * P:(t + 1) * P], ones[:],
                                                    start=True, stop=True)
                        last.then_inc(n2_ready, 1)
                    if j == 6 and do_f:
                        feed_forward(1, 0, 3)
                    if j == 6 and do_c:
                        pe.wait_ge(rn_done, c + 1)
                        pe.wait_ge(og_done, 2 * (c + 1))
                        for t in range(TC):
                            last = nc.tensor.transpose(ps_o[t // 4][:, (t % 4) * P:(t % 4 + 1) * P],
                                                       rn[:, t:t + 1].to_broadcast([P, P]), ident[:])
                            if t % 4 == 3:
                                last.then_inc(rb_ready, 1)
                    if j == 7 and do_f:
                        feed_forward(1, 3, TC)
                    if j == 7 and do_a:
                        if do_c:
                            pe.wait_ge(att_done, 2 * (c + 1))
                        for h in range(2):
                            for t in range(4):
                                tok = (4 * h + t) * P
                                last = nc.tensor.transpose(ps_o[h][:, t * P:(t + 1) * P],
                                                           c_in[s][:, tok:tok + P], ident[:])
                            last.then_inc(tc_ready, 1)
                    if 2 <= j < 6 and do_a:
                        pe.wait_ge(tk_moved, 8 * a + 2 * (j - 2) + 2)
                    if j < 4 and do_c:
                        transpose_q(c, j + 4)
                    if j >= 4 and do_a:
                        transpose_q(a, j - 4)

            pipeline(pe, iteration)



_INS = ["x", "ctx_4096", "L0_xattn_Wq", "L0_xattn_Wk", "L0_xattn_Wv", "L0_xattn_Wo", "L0_xattn_bo", "L0_xattn_g",
        "L0_ffn_qweight", "L0_ffn_scales", "L0_ffn_zeros", "L0_ffn_bias"]


def kernel(**inputs):
    import concourse.bacc as bacc
    from concourse.bass_utils import run_bass_kernel_spmd

    nc = bacc.Bacc("TRN2", target_bir_lowering=False, num_devices=1)
    arrays, args = {}, []
    for name in _INS:
        a = np.ascontiguousarray(inputs[name])
        arrays[f"in_{name}"] = a
        args.append(nc.dram_tensor(f"in_{name}", a.shape, mybir.dt.from_np(a.dtype), kind="ExternalInput").ap())
    out = nc.dram_tensor("out_x", inputs["x"].shape, F32, kind="ExternalOutput").ap()
    build(nc, *args, out)
    r = run_bass_kernel_spmd(nc, [arrays], core_ids=[0])
    return r.results[0]["out_x"]
```

```python
from contextlib import ExitStack

import numpy as np

import concourse.bass as bass
from concourse import mybir

F32 = mybir.dt.float32
F32R = mybir.dt.float32r
F16 = mybir.dt.float16
I32 = mybir.dt.int32
ALU = mybir.AluOpType
ACT = mybir.ActivationFunctionType
AX_X = mybir.AxisListType.X

P = 128
BANK = 512
STEPS = 8
LN_EPS = 1e-5
NORM_FLOOR_SQ = 1e-24
ROUND = 1.5 * 2.0 ** 23


def build(nc, x, ctx_in, wq, wk, wv, wo, bo, g, qweight, scales, zeros, bias, out):
    NB, DIM, N = x.shape
    HID = wq.shape[0]
    DH = 64
    HEADS = HID // DH
    HC = HID // P
    TC = N // P
    HALVES = N // BANK
    OUT = qweight.shape[1]
    RC = qweight.shape[0] // P
    assert DIM == P and TC == STEPS and HC == 4 and OUT == N and 2 * RC == TC
    q_scale = DH ** -0.5
    g_scale = float(np.sqrt(DIM))

    with ExitStack() as ctx:
        def sb(name, shape, dt=F32):
            return ctx.enter_context(nc.sbuf_tensor(name, shape, dt))

        def psum(name, shape):
            return ctx.enter_context(nc.psum_tensor(name, shape, F32))

        def sem(name):
            return ctx.enter_context(nc.semaphore(name))

        ident = sb("ident", [P, P])
        ones = sb("ones", [P, 1])
        neg_half = sb("neg_half", [P, TC])
        eps_col = sb("eps_col", [P, 1])
        minus_col = sb("minus_col", [P, 1])
        wq_hi = sb("wq_hi", [P, HID], F32R)
        wq_lo = sb("wq_lo", [P, HID], F32R)
        wk_hi = sb("wk_hi", [P, HID], F32R)
        wk_lo = sb("wk_lo", [P, HID], F32R)
        vo = sb("vo", [P, HEADS * P])
        w_int = sb("w_int", [P, 2, RC, OUT], F16)
        scale_bc = sb("scale_bc", [P, OUT])
        zero_bc = sb("zero_bc", [P, OUT])
        bias_bc = sb("bias_bc", [P, OUT])
        bo_col = sb("bo_col", [P, 1])
        gs_col = sb("gs_col", [P, 1])
        bogs_col = sb("bogs_col", [P, 1])

        x_in = [sb(f"x_in{s}", [P, N]) for s in range(2)]
        c_in = [sb(f"c_in{s}", [P, N]) for s in range(2)]
        x_res = sb("x_res", [P, N])
        xn = sb("xn", [P, N])
        xn_hi = [sb(f"xn_hi{s}", [P, N], F32R) for s in range(2)]
        xn_lo = [sb(f"xn_lo{s}", [P, N], F32R) for s in range(2)]
        c_hi = sb("c_hi", [P, N], F32R)
        c_lo = sb("c_lo", [P, N], F32R)
        c_t = sb("c_t", [P, TC, P])
        stats1 = sb("stats1", [P, 2, 6])
        mv1 = sb("mv1", [P, 2])
        ve1 = sb("ve1", [P, 1])
        rstd1 = sb("rstd1", [P, 1])
        QR = 8
        q_exp = sb("q_exp", [P, QR, HID])
        q_nmax = sb("q_nmax", [P, QR, HEADS])
        q_sum = sb("q_sum", [P, QR, HEADS])
        q_rec = sb("q_rec", [P, QR, HEADS])
        k_exp = sb("k_exp", [P, 2, N])
        k_nmax = sb("k_nmax", [P, HC])
        k_sum = sb("k_sum", [P, 2, HC])
        k_rec = sb("k_rec", [P, HC])
        k_t = sb("k_t", [P, TC, HID])
        q_hi = sb("q_hi", [P, HC, N], F32R)
        q_lo = sb("q_lo", [P, HC, N], F32R)
        m_t = sb("m_t", [P, HID])
        g_t = sb("g_t", [P, HC, P])
        g_hi = sb("g_hi", [P, HC, P], F32R)
        g_lo = sb("g_lo", [P, HC, P], F32R)
        og = sb("og", [P, N])
        sq = sb("sq", [P, N])
        n2 = sb("n2", [P, TC])
        rn = sb("rn", [P, TC])
        x2 = sb("x2", [P, N])
        stats2 = sb("stats2", [P, 2, 6])
        mv2 = sb("mv2", [P, 2])
        ve2 = sb("ve2", [P, 1])
        rstd2 = sb("rstd2", [P, 1])
        nm2 = sb("nm2", [P, 1])
        nmr2 = sb("nmr2", [P, 1])
        rs2 = sb("rs2", [P, 1])
        nrs2 = sb("nrs2", [P, 1])
        x2n = og[:].rearrange("p (t r) -> p t r", t=2)
        x2b = sb("x2b", [P, N])
        x2_hi = sb("x2_hi", [P, TC, P], F16)
        x2_lo = sb("x2_lo", [P, TC, P], F16)
        y = sb("y", [P, OUT])

        q_packed = [t[:].bitcast(I32) for t in (og, sq, x2b, x2)]
        q_nibble = [t[:].bitcast(I32) for t in (y, x_res)]
        rows_in = sb("rows_in", [TC, 3, P])
        inv_scale = sb("inv_scale", [TC, P])
        cols = sb("cols", [P, 3, TC])
        k_flat = k_t[:].rearrange("p t h -> p (t h)")
        wq_in = k_flat[:, 0:HID].rearrange("p (k c) -> p k c", k=HC)
        wk_in = k_flat[:, HID:2 * HID].rearrange("p (k c) -> p k c", k=HC)
        wv_in = k_flat[:, 2 * HID:3 * HID].rearrange("p (k c) -> p k c", k=HC)
        wo_in = k_flat[:, 3 * HID:4 * HID]
        wo_t = k_flat[:, 4 * HID:5 * HID].rearrange("p (k o) -> p k o", k=HC)

        ps_q = psum("ps_q", [P, BANK])
        ps_k = psum("ps_k", [P, HALVES * BANK])
        ps_ta = psum("ps_ta", [P, BANK])
        ps_tb = psum("ps_tb", [P, BANK])
        ps_m = psum("ps_m", [P, BANK])
        ps_o = [psum(f"ps_o{h}", [P, BANK]) for h in range(2)]

        wqk_loaded = sem("wqk_loaded")
        wvo_loaded = sem("wvo_loaded")
        rows_loaded = sem("rows_loaded")
        qw_loaded = sem("qw_loaded")
        consts_made = sem("consts_made")
        gs_done = sem("gs_done")
        wt_ready = sem("wt_ready")
        whi_done = sem("whi_done")
        wlo_done = sem("wlo_done")
        wot_moved = sem("wot_moved")
        vo_ready = sem("vo_ready")
        vo_moved = sem("vo_moved")
        bogs_done = sem("bogs_done")
        zero_steps = sem("zero_steps")
        cols_ready = sem("cols_ready")
        cols_moved = sem("cols_moved")
        rows_ready = sem("rows_ready")
        rows_moved = sem("rows_moved")
        nibble_done = sem("nibble_done")
        w_converted = sem("w_converted")
        x_loaded = [sem(f"x_loaded{s}") for s in range(2)]
        c_loaded = [sem(f"c_loaded{s}") for s in range(2)]
        xres_loaded = sem("xres_loaded")
        y_stored = sem("y_stored")
        stats1_part = sem("stats1_part")
        stats1_done = sem("stats1_done")
        ve1_done = sem("ve1_done")
        rstd1_done = sem("rstd1_done")
        xn_done = sem("xn_done")
        xnhi_done = sem("xnhi_done")
        xnlo_done = sem("xnlo_done")
        chi_done = sem("chi_done")
        clo_done = sem("clo_done")
        q_ready = sem("q_ready")
        k_ready = sem("k_ready")
        qmax_done = sem("qmax_done")
        qsub_done = sem("qsub_done")
        qexp_done = sem("qexp_done")
        qsum_done = sem("qsum_done")
        qrec_done = sem("qrec_done")
        qs_done = sem("qs_done")
        tq_ready = sem("tq_ready")
        tq_moved = sem("tq_moved")
        qlo_done = sem("qlo_done")
        kmax_done = sem("kmax_done")
        kexp_done = sem("kexp_done")
        tk_ready = sem("tk_ready")
        tk_moved = sem("tk_moved")
        tc_ready = sem("tc_ready")
        tc_moved = sem("tc_moved")
        m_ready = sem("m_ready")
        m_moved = sem("m_moved")
        krec_done = sem("krec_done")
        g_ready = sem("g_ready")
        g_moved = sem("g_moved")
        ghi_done = sem("ghi_done")
        glo_done = sem("glo_done")
        out_ready = sem("out_ready")
        og_done = sem("og_done")
        sq_done = sem("sq_done")
        n2_ready = sem("n2_ready")
        n2_moved = sem("n2_moved")
        rn_done = sem("rn_done")
        rb_ready = sem("rb_ready")
        att_done = sem("att_done")
        x2_done = sem("x2_done")
        stats2_part = sem("stats2_part")
        stats2_done = sem("stats2_done")
        rstd2_steps = sem("rstd2_steps")
        x2n_done = sem("x2n_done")
        nrs_done = sem("nrs_done")
        x2b_done = sem("x2b_done")
        x2c_done = sem("x2c_done")
        tx_ready = sem("tx_ready")
        x2hi_done = sem("x2hi_done")
        x2lo_done = sem("x2lo_done")
        y_ready = sem("y_ready")
        ymul_done = sem("ymul_done")
        y_done = sem("y_done")

        def begun(value):
            return not isinstance(value, int) or value > 0

        def loads(b, s):
            return 8 * (b - s) + 16

        FIRST, LAST = -1, NB + 2
        LOOP = (3, NB - 1)

        def pipeline(eng, iteration, end=LOOP[1]):
            def peeled(i):
                iteration(i, i % 2, i + 1 < NB, 0 <= i < NB, 0 <= i - 1 < NB, 0 <= i - 2 < NB)

            for i in range(FIRST, LOOP[0]):
                peeled(i)
            with eng.Fori(LOOP[0], end, 2) as i:
                iteration(i, LOOP[0] % 2, True, True, True, True)
                iteration(i + 1, (LOOP[0] + 1) % 2, True, True, True, True)
            for i in range(end, LAST):
                peeled(i)

        def halves(ap):
            return [ap[:, h * BANK:(h + 1) * BANK] for h in range(HALVES)]

        block = ctx.enter_context(nc.Block())

        @block.sync
        def _(sp):
            def load_x(b, s):
                sp.dma_start(x_in[s][:], x[b]).then_inc(x_loaded[s], 16)

            def load_c(b, s):
                sp.dma_start(c_in[s][:], ctx_in[b]).then_inc(c_loaded[s], 16)

            load_x(0, 0)
            sp.dma_start(wq_in, wq.rearrange("(k p) c -> p k c", p=P)).then_inc(wqk_loaded, 16)
            sp.dma_start(wk_in, wk.rearrange("(k p) c -> p k c", p=P)).then_inc(wqk_loaded, 16)
            load_c(0, 0)
            for dst, src in (
                (wo_in, wo),
                (wv_in, wv.rearrange("(k p) c -> p k c", p=P)),
                (bo_col[:], bo.rearrange("(p a) -> p a", a=1)),
                (gs_col[:], g.rearrange("a p b -> (a p) b")),
            ):
                sp.dma_start(dst, src).then_inc(wvo_loaded, 16)
            for k, src in enumerate((scales.rearrange("(t p) a -> t (p a)", p=P),
                                     zeros.rearrange("(t p) a -> t (p a)", p=P),
                                     bias.rearrange("(t p) -> t p", p=P))):
                sp.dma_start(rows_in[:, k, :], src).then_inc(rows_loaded, 16)
            for m in range(RC):
                sp.dma_start(q_packed[m], qweight[m * P:(m + 1) * P, :]).then_inc(qw_loaded, 16)
            load_x(1, 1)
            load_c(1, 1)

            def kept(value):
                return value if isinstance(value, int) else sp.snap(value)

            def iteration(i, s, do_n, do_a, do_c, do_f):
                c, f = i - 1, i - 2
                if do_c:
                    before = kept(2 * c)
                    if isinstance(i, int) and i == 1:
                        sp.wait_ge(w_converted, 2 * RC)
                    sp.wait_ge(wqk_loaded, 32)
                    if begun(c):
                        sp.wait_ge(x2_done, before)
                    sp.dma_start(x_res[:], x[c]).then_inc(xres_loaded, 16)
                if not isinstance(i, int) or 0 <= i < NB - 2:
                    after, twice = kept(i + 1), kept(2 * (i + 1))
                    sp.wait_ge(wqk_loaded, 32)
                    sp.wait_ge(xn_done, after)
                    sp.dma_start(x_in[s][:], x[i + 2]).then_inc(x_loaded[s], 16)
                    sp.wait_ge(wqk_loaded, 32)
                    sp.wait_ge(chi_done, after)
                    sp.wait_ge(clo_done, after)
                    sp.wait_ge(tc_ready, twice)
                    sp.dma_start(c_in[s][:], ctx_in[i + 2]).then_inc(c_loaded[s], 16)
                if isinstance(i, int) and f == NB - 1:
                    for h in range(2):
                        sp.wait_ge(y_done, 2 * f + h + 1)
                        sp.dma_start(halves(out[f])[h], halves(y)[h]).then_inc(y_stored, 16)
                elif do_f:
                    finished = kept(2 * (f + 1))
                    sp.wait_ge(wqk_loaded, 32)
                    sp.wait_ge(y_done, finished)
                    sp.dma_start(out[f], y[:]).then_inc(y_stored, 16)

            pipeline(sp, iteration, end=NB - 3)
            sp.wait_ge(y_stored, 16 * (NB + 1))

        @block.gpsimd
        def _(pool):
            nc.gpsimd.memset(ident[:], 0.0).then_inc(consts_made, 1)
            nc.gpsimd.memset(ones[:], 1.0).then_inc(consts_made, 1)
            nc.gpsimd.memset(neg_half[:], -0.5).then_inc(consts_made, 1)
            nc.gpsimd.memset(eps_col[:], LN_EPS).then_inc(consts_made, 1)
            nc.gpsimd.memset(minus_col[:], -1.0).then_inc(consts_made, 1)
            pool.wait_ge(consts_made, 5)
            nc.gpsimd.affine_select(out=ident[:], in_=ident[:], compare_op=ALU.not_equal, fill=1.0,
                                    base=0, pattern=[[-1, P]], channel_multiplier=1).then_inc(consts_made, 1)

            def iteration(i, s, do_n, do_a, do_c, do_f):
                n, a, c, f = i + 1, i, i - 1, i - 2

                def scale_q(b, j):
                    pool.wait_ge(qrec_done, 8 * b + j + 1)
                    chunk = q_exp[:, j, :].rearrange("p (h d) -> p h d", h=HEADS)
                    rec = q_rec[:, j, :].unsqueeze(2).to_broadcast([P, HEADS, DH])
                    nc.gpsimd.tensor_tensor(chunk, chunk, rec, ALU.mult).then_inc(qs_done, 1)

                def add_y(h):
                    pool.wait_ge(ymul_done, 2 * f + h + 1)
                    pool.wait_ge(x2c_done, f + 1)
                    nc.gpsimd.tensor_tensor(halves(y)[h], halves(y)[h], halves(x2b)[h], ALU.add).then_inc(y_done, 1)

                for j in range(STEPS):
                    if j == 7 and do_c:
                        for h in range(HALVES):
                            pool.wait_ge(att_done, 2 * c + h + 1)
                            if h == 0:
                                pool.wait_ge(xres_loaded, 16 * (c + 1))
                                if begun(c):
                                    pool.wait_ge(x2n_done, c)
                            nc.gpsimd.tensor_tensor(halves(x2)[h], halves(og)[h], halves(x_res)[h],
                                                    ALU.add).then_inc(x2_done, 1)
                    if j == 0 and do_c:
                        scale_q(c, STEPS - 1)
                    if j == 0 and do_f:
                        pool.wait_ge(stats2_done, f + 1)
                        nc.gpsimd.tensor_tensor(ve2[:], mv2[:, 1:2], eps_col[:], ALU.add).then_inc(rstd2_steps, 1)
                        nc.gpsimd.tensor_tensor(nm2[:], mv2[:, 0:1], minus_col[:], ALU.mult).then_inc(rstd2_steps, 1)
                        pool.wait_ge(rstd2_steps, 4 * f + 1)
                        nc.gpsimd.tensor_tensor(rstd2[:], ve2[:], neg_half[:, 0:1], ALU.pow).then_inc(rstd2_steps, 1)
                        pool.wait_ge(rstd2_steps, 4 * f + 3)
                        nc.gpsimd.tensor_tensor(nmr2[:], nm2[:], rstd2[:], ALU.mult).then_inc(rstd2_steps, 1)
                    if j >= 1 and do_a:
                        scale_q(a, j - 1)
                    if j in (6, 7) and do_f:
                        add_y(j - 6)
                    if j == 1 and do_f:
                        if isinstance(i, int) and i == 2:
                            pool.wait_ge(rows_moved, 6)
                        if begun(2 * f):
                            pool.wait_ge(y_done, 2 * f)
                        pool.wait_ge(x2_done, 2 * (f + 1))
                        nc.gpsimd.tensor_tensor(x2b[:], x2[:], bias_bc[:], ALU.add).then_inc(x2b_done, 1)
                    if j == 4 and do_n:
                        pool.wait_ge(stats1_done, n + 1)
                        nc.gpsimd.tensor_tensor(ve1[:], mv1[:, 1:2], eps_col[:], ALU.add).then_inc(ve1_done, 1)
                        pool.wait_ge(ve1_done, n + 1)
                        nc.gpsimd.tensor_tensor(rstd1[:], ve1[:], neg_half[:, 0:1], ALU.pow).then_inc(rstd1_done, 1)
                    if j == 4 and do_n:
                        pool.wait_ge(chi_done, n + 1)
                        nc.gpsimd.tensor_tensor(c_lo[:], c_in[1 - s][:], c_hi[:].bitcast(F32),
                                                ALU.subtract).then_inc(clo_done, 1)
                    if j == 6 and do_n:
                        pool.wait_ge(xnhi_done, n + 1)
                        if begun(8 * a):
                            pool.wait_ge(q_ready, 8 * a)
                        nc.gpsimd.tensor_tensor(xn_lo[1 - s][:], xn[:], xn_hi[1 - s][:].bitcast(F32),
                                                ALU.subtract).then_inc(xnlo_done, 1)
                    if j == 5 and do_c:
                        pool.wait_ge(n2_moved, c + 1)
                        nc.gpsimd.tensor_tensor(rn[:], n2[:], neg_half[:], ALU.pow).then_inc(rn_done, 1)

            pipeline(pool, iteration)

        @block.scalar
        def _(act):
            def set_up():
                act.wait_ge(wt_ready, 1)
                nc.scalar.activation(wk_hi[:], ps_ta[:], ACT.Copy).then_inc(whi_done, 1)
                nc.scalar.activation(wq_hi[:], ps_q[:], ACT.Copy).then_inc(whi_done, 1)
                act.wait_ge(wt_ready, 2)
                nc.scalar.activation(wo_t, ps_tb[:].rearrange("p (k o) -> p k o", k=HC),
                                     ACT.Copy).then_inc(wot_moved, 1)
                act.wait_ge(wvo_loaded, 64)
                nc.scalar.mul(gs_col[:], gs_col[:], g_scale).then_inc(gs_done, 1)

            def convert_nibble(k):
                act.wait_ge(nibble_done, k + 1)
                nc.scalar.activation(w_int[:, k // RC, k % RC], q_nibble[k % 2], ACT.Copy).then_inc(w_converted, 1)

            def set_up_ffn(j):
                if j == 0:
                    act.wait_ge(cols_ready, 1)
                    nc.scalar.activation(cols[:].rearrange("p k t -> p (k t)"), ps_m[:, 0:3 * TC],
                                         ACT.Copy).then_inc(cols_moved, 1)
                if 1 <= j < 7:
                    act.wait_ge(rows_ready, j)
                    row = (scale_bc, zero_bc, bias_bc)[(j - 1) // 2]
                    nc.scalar.activation(halves(row)[(j - 1) % 2], ps_m[:], ACT.Copy).then_inc(rows_moved, 1)
                if j > 0:
                    convert_nibble(j - 1)

            def iteration(i, s, do_n, do_a, do_c, do_f):
                n, a, c, f = i + 1, i, i - 1, i - 2

                def exp_k(j):
                    act.wait_ge(kmax_done, 4 * a + j + 1)
                    if begun(8 * a + 2 * (j - 2) + 2):
                        act.wait_ge(tk_ready, 8 * a + 2 * (j - 2) + 2)
                    nc.scalar.activation(k_exp[:, j % 2, :], ps_k[:], ACT.Exp, bias=k_nmax[:, j:j + 1],
                                         accum_out=k_sum[:, s, j:j + 1]).then_inc(kexp_done, 1)

                def exp_q(j):
                    act.wait_ge(qsub_done, 8 * a + j + 1)
                    nc.scalar.activation(q_exp[:, j, :], q_exp[:, j, :], ACT.Exp).then_inc(qexp_done, 1)

                def move_tq(b, j):
                    act.wait_ge(tq_ready, 8 * b + j + 1)
                    if begun(2 * (b - 1) + j // 4 + 1):
                        act.wait_ge(out_ready, 2 * (b - 1) + j // 4 + 1)
                    nc.scalar.activation(q_hi[:, :, j * P:(j + 1) * P],
                                         ps_tb[:].rearrange("p (c t) -> p c t", c=HC),
                                         ACT.Copy).then_inc(tq_moved, 1)

                def move_tk(k):
                    t0, fc = 4 * (k % 2), k // 2
                    act.wait_ge(tk_ready, 8 * a + k + 1)
                    if k == 0 and begun(a):
                        act.wait_ge(m_ready, a)
                    nc.scalar.activation(k_t[:, t0:t0 + 4, fc * P:(fc + 1) * P],
                                         (ps_ta, ps_tb)[k % 2][:].rearrange("p (t c) -> p t c", t=4),
                                         ACT.Copy).then_inc(tk_moved, 1)

                def squares(h):
                    if isinstance(i, int) and i == 1 and h == 0:
                        act.wait_ge(bogs_done, 1)
                    act.wait_ge(out_ready, 2 * c + h + 1)
                    if h == 0 and begun(c):
                        act.wait_ge(n2_ready, c)
                    nc.scalar.activation(halves(sq)[h], ps_o[h][:], ACT.Square, bias=bo_col[:]).then_inc(sq_done, 1)
                    if do_f and h == 0:
                        act.wait_ge(tx_ready, 2 * (f + 1))
                    nc.scalar.activation(halves(og)[h], ps_o[h][:], ACT.Identity, bias=bogs_col[:],
                                         scale=gs_col[:]).then_inc(og_done, 1)

                if isinstance(i, int) and i == 0:
                    set_up()
                for j in range(STEPS):
                    if j <= 4 and do_c:
                        move_tq(c, j + 3)
                    if j == 3 and do_c:
                        act.wait_ge(g_moved, c + 1)
                        if begun(2 * c):
                            act.wait_ge(out_ready, 2 * c)
                        nc.scalar.activation(g_hi[:], g_t[:], ACT.Copy).then_inc(ghi_done, 1)
                    if j >= 5 and do_a:
                        move_tq(a, j - 5)
                    if j == 5 and do_c:
                        squares(1)
                    if 2 <= j < 6 and do_a:
                        move_tk(2 * (j - 2))
                        move_tk(2 * (j - 2) + 1)
                    if j == 1 and do_f:
                        act.wait_ge(rstd2_steps, 4 * (f + 1))
                        if begun(f):
                            act.wait_ge(nrs_done, f)
                        nc.scalar.activation(x2n, x2[:].rearrange("p (r t) -> p t r", t=2), ACT.Identity,
                                             bias=nmr2[:], scale=rstd2[:], accum_out=rs2[:]).then_inc(x2n_done, 1)
                    if j < HC and do_a:
                        exp_k(j)
                    if do_a:
                        exp_q(j)
                    if j == 1 and do_f:
                        for h in range(2):
                            act.wait_ge(tx_ready, 2 * f + h + 1)
                            if h == 0 and begun(2 * f):
                                act.wait_ge(y_ready, 2 * f)
                            nc.scalar.activation(x2_hi[:, 4 * h:4 * h + 4, :],
                                                 ps_o[h][:].rearrange("p (t c) -> p t c", t=4),
                                                 ACT.Copy).then_inc(x2hi_done, 1)
                    if j == 1 and do_c:
                        act.wait_ge(m_ready, c + 1)
                        if begun(c):
                            act.wait_ge(g_ready, c)
                        nc.scalar.activation(m_t[:], ps_m[:], ACT.Copy).then_inc(m_moved, 1)
                    if j == 4 and do_c:
                        squares(0)
                    if j == 4 and do_n:
                        act.wait_ge(c_loaded[1 - s], loads(n, 1 - s))
                        if begun(8 * n):
                            act.wait_ge(k_ready, 8 * n)
                        nc.scalar.activation(c_hi[:], c_in[1 - s][:], ACT.Copy).then_inc(chi_done, 1)
                    if j == 5 and do_n:
                        act.wait_ge(xn_done, n + 1)
                        if begun(8 * a):
                            act.wait_ge(q_ready, 8 * a)
                        nc.scalar.activation(xn_hi[1 - s][:], xn[:], ACT.Copy).then_inc(xnhi_done, 1)
                    if j == 7 and do_a:
                        for h in range(2):
                            act.wait_ge(tc_ready, 2 * a + h + 1)
                            nc.scalar.activation(c_t[:, 4 * h:4 * h + 4, :],
                                                 ps_o[h][:].rearrange("p (t c) -> p t c", t=4),
                                                 ACT.Copy).then_inc(tc_moved, 1)
                    if isinstance(i, int) and i == 0:
                        set_up_ffn(j)
                    if isinstance(i, int) and i == 1 and j == 0:
                        convert_nibble(2 * RC - 1)

            pipeline(act, iteration)

        @block.vector
        def _(dve):
            def set_up():
                dve.wait_ge(whi_done, 1)
                nc.vector.tensor_tensor(wk_lo[:], ps_ta[:], wk_hi[:].bitcast(F32), ALU.subtract).then_inc(wlo_done, 1)
                dve.wait_ge(whi_done, 2)
                nc.vector.tensor_tensor(wq_lo[:], ps_q[:], wq_hi[:].bitcast(F32), ALU.subtract).then_inc(wlo_done, 1)
                dve.wait_ge(rows_loaded, 48)
                scale, zero = rows_in[:, 0, :], rows_in[:, 1, :]
                nc.vector.reciprocal(inv_scale[:], scale).then_inc(zero_steps, 1)
                dve.wait_ge(zero_steps, 1)
                nc.vector.tensor_tensor(zero, zero, inv_scale[:], ALU.mult).then_inc(zero_steps, 1)
                dve.wait_ge(zero_steps, 2)
                nc.vector.tensor_scalar(zero, zero, ROUND, ROUND, ALU.add, ALU.subtract).then_inc(zero_steps, 1)
                dve.wait_ge(zero_steps, 3)
                nc.vector.tensor_tensor(zero, zero, scale, ALU.mult).then_inc(zero_steps, 1)

            def set_up_late(k):
                if k == 0:
                    dve.wait_ge(vo_ready, 1)
                    for q in range(2):
                        nc.vector.tensor_copy(vo[:].rearrange("p (k q o) -> p q k o", q=2, o=P)[:, q],
                                              ps_o[q][:].rearrange("p (k o) -> p k o", k=HC)).then_inc(vo_moved, 1)
                    dve.wait_ge(gs_done, 1)
                    nc.vector.tensor_tensor(bogs_col[:], bo_col[:], gs_col[:], ALU.mult).then_inc(bogs_done, 1)
                    dve.wait_ge(qw_loaded, 16 * RC)
                elif k > 1:
                    dve.wait_ge(w_converted, k - 1)
                nc.vector.tensor_scalar(q_nibble[k % 2], q_packed[k % RC], 4 * (k // RC), 15, ALU.logical_shift_right,
                                        ALU.bitwise_and).then_inc(nibble_done, 1)

            def iteration(i, s, do_n, do_a, do_c, do_f):
                n, a, c, f = i + 1, i, i - 1, i - 2

                def max_k(j):
                    dve.wait_ge(k_ready, 8 * a + 2 * j + 2)
                    if begun(4 * (a - 1) + j + 1):
                        dve.wait_ge(kexp_done, 4 * (a - 1) + j + 1)
                    nc.vector.tensor_reduce(k_nmax[:, j:j + 1], ps_k[:], op=ALU.max, axis=AX_X,
                                            negate=True).then_inc(kmax_done, 1)

                def shift_q(j):
                    heads = ps_q[:].rearrange("p (h d) -> p h d", h=HEADS)
                    dve.wait_ge(q_ready, 8 * a + j + 1)
                    nc.vector.tensor_reduce(q_nmax[:, j, :], heads, op=ALU.max, axis=AX_X,
                                            negate=True).then_inc(qmax_done, 1)
                    dve.wait_ge(qmax_done, 8 * a + j + 1)
                    if begun(8 * (a - 1) + j + 1):
                        dve.wait_ge(tq_ready, 8 * (a - 1) + j + 1)
                    nc.vector.tensor_tensor(q_exp[:, j, :].rearrange("p (h d) -> p h d", h=HEADS), heads,
                                            q_nmax[:, j, :].unsqueeze(2).to_broadcast([P, HEADS, DH]),
                                            ALU.add).then_inc(qsub_done, 1)

                def sum_q(b, j):
                    dve.wait_ge(qexp_done, 8 * b + j + 1)
                    nc.vector.tensor_reduce(q_sum[:, j, :], q_exp[:, j, :].rearrange("p (h d) -> p h d", h=HEADS),
                                            op=ALU.add, axis=AX_X).then_inc(qsum_done, 1)
                    dve.wait_ge(qsum_done, 8 * b + j + 1)
                    nc.vector.reciprocal(q_rec[:, j, :], q_sum[:, j, :]).then_inc(qrec_done, 1)

                def low_q(b, j):
                    dve.wait_ge(tq_moved, 8 * b + j + 1)
                    nc.vector.tensor_tensor(q_lo[:, :, j * P:(j + 1) * P],
                                            ps_tb[:].rearrange("p (c t) -> p c t", c=HC),
                                            q_hi[:, :, j * P:(j + 1) * P].bitcast(F32),
                                            ALU.subtract).then_inc(qlo_done, 1)

                def scale_y(h):
                    dve.wait_ge(y_ready, 2 * f + h + 1)
                    if h == 0 and begun(16 * f):
                        dve.wait_ge(y_stored, 16 * f)
                    ps_y = ps_q if h == 1 and not do_a else ps_m
                    nc.vector.tensor_tensor(halves(y)[h], ps_y[:], halves(scale_bc)[h],
                                            ALU.mult).then_inc(ymul_done, 1)

                if isinstance(i, int) and i == 0:
                    set_up()
                for j in range(STEPS):
                    if j in (0, 1, 2, 4) and do_c:
                        low_q(c, j + 3)
                    if j >= 5 and do_a:
                        low_q(a, j - 5)
                    if j < HC and do_a:
                        max_k(j)
                    if do_a:
                        shift_q(j)
                    if j == 4 and do_n:
                        dve.wait_ge(x_loaded[1 - s], loads(n, 1 - s))
                        if begun(n):
                            dve.wait_ge(ve1_done, n)
                            dve.wait_ge(xn_done, n)
                        for h in range(HALVES):
                            nc.vector.bn_stats(stats1[:, h, :], halves(x_in[1 - s])[h]).then_inc(stats1_part, 1)
                        dve.wait_ge(stats1_part, 2 * (n + 1))
                    if j == 7 and do_f:
                        scale_y(1)
                    if j == 0 and do_f:
                        if begun(4 * f):
                            dve.wait_ge(rstd2_steps, 4 * f)
                        for h in range(HALVES):
                            dve.wait_ge(x2_done, 2 * f + h + 1)
                            nc.vector.bn_stats(stats2[:, h, :], halves(x2)[h]).then_inc(stats2_part, 1)
                        dve.wait_ge(stats2_part, 2 * (f + 1))
                    if j == 2 and do_c:
                        dve.wait_ge(krec_done, 2 * c + 2)
                        dve.wait_ge(g_ready, c + 1)
                        nc.vector.tensor_tensor(g_t[:], ps_o[0][:].rearrange("p (c o) -> p c o", c=HC),
                                                k_rec[:].unsqueeze(2).to_broadcast([P, HC, P]),
                                                ALU.mult).then_inc(g_moved, 1)
                        low_q(c, 6)
                        dve.wait_ge(ghi_done, c + 1)
                        nc.vector.tensor_tensor(g_lo[:], g_t[:], g_hi[:].bitcast(F32),
                                                ALU.subtract).then_inc(glo_done, 1)
                    if j == 0 and do_c:
                        sum_q(c, STEPS - 1)
                    if j >= 1 and j != 2 and do_a:
                        if j == 3:
                            sum_q(a, 1)
                        sum_q(a, j - 1)
                    if j == 4 and do_n:
                        nc.vector.bn_aggr(mv1[:], stats1[:].rearrange("p a b -> p (a b)")).then_inc(stats1_done, 1)
                    if j == 0 and do_f:
                        nc.vector.bn_aggr(mv2[:], stats2[:].rearrange("p a b -> p (a b)")).then_inc(stats2_done, 1)
                    if j == 1 and do_f:
                        for h in range(2):
                            dve.wait_ge(x2hi_done, 2 * f + h + 1)
                            nc.vector.tensor_tensor(x2_lo[:, 4 * h:4 * h + 4, :],
                                                    ps_o[h][:].rearrange("p (t c) -> p t c", t=4),
                                                    x2_hi[:, 4 * h:4 * h + 4, :],
                                                    ALU.subtract).then_inc(x2lo_done, 1)
                    if j == 5 and do_n:
                        dve.wait_ge(rstd1_done, n + 1)
                        if begun(n):
                            dve.wait_ge(xnhi_done, n)
                            dve.wait_ge(xnlo_done, n)
                        nc.vector.tensor_scalar(xn[:], x_in[1 - s][:], mv1[:, 0:1], rstd1[:], ALU.subtract,
                                                ALU.mult).then_inc(xn_done, 1)
                    if j == 4 and do_f:
                        if isinstance(i, int) and i == 2:
                            dve.wait_ge(rows_moved, 6)
                        dve.wait_ge(x2n_done, f + 1)
                        nc.vector.tensor_scalar(nrs2[:], rs2[:], -1.0, None, ALU.mult).then_inc(nrs_done, 1)
                        dve.wait_ge(nrs_done, f + 1)
                        dve.wait_ge(x2b_done, f + 1)
                        nc.vector.scalar_tensor_tensor(out=x2b[:], in0=zero_bc[:], scalar=nrs2[:], in1=x2b[:],
                                                       op0=ALU.mult, op1=ALU.add).then_inc(x2c_done, 1)
                    if j == 5 and do_c:
                        dve.wait_ge(n2_ready, c + 1)
                        if begun(c):
                            dve.wait_ge(rn_done, c)
                        nc.vector.tensor_scalar(n2[:], ps_ta[:, 0:TC], NORM_FLOOR_SQ, None,
                                                ALU.max).then_inc(n2_moved, 1)
                    if j == 5 and do_f:
                        scale_y(0)
                    if j == 6 and do_c:
                        for h in range(HALVES):
                            dve.wait_ge(rb_ready, 2 * c + h + 1)
                            dve.wait_ge(og_done, 2 * c + h + 1)
                            nc.vector.tensor_tensor(halves(og)[h], halves(og)[h], ps_o[h][:],
                                                    ALU.mult).then_inc(att_done, 1)
                    if j == 5 and do_a:
                        dve.wait_ge(kexp_done, 4 * (a + 1))
                        nc.vector.reciprocal(k_rec[:], k_sum[:, s, :]).then_inc(krec_done, 1)
                        dve.wait_ge(krec_done, 2 * a + 1)
                        nc.vector.tensor_scalar(k_rec[:], k_rec[:], q_scale, None, ALU.mult).then_inc(krec_done, 1)
                    if isinstance(i, int) and i == 0:
                        set_up_late(j)

            pipeline(dve, iteration)

        @block.tensor
        def _(pe):
            pe.wait_ge(consts_made, 6)
            pe.wait_ge(wqk_loaded, 32)
            for w, ps in ((wk_in, ps_ta), (wq_in, ps_q)):
                for k in range(HC):
                    last = nc.tensor.transpose(ps[:, k * P:(k + 1) * P], w[:, k, :], ident[:])
            last.then_inc(wt_ready, 1)
            pe.wait_ge(wvo_loaded, 64)
            for k in range(HC):
                last = nc.tensor.transpose(ps_tb[:, k * P:(k + 1) * P], wo_in[:, k * P:(k + 1) * P], ident[:])
            last.then_inc(wt_ready, 1)
            pe.wait_ge(wlo_done, 2)

            def set_up_vo():
                pe.wait_ge(wot_moved, 1)
                for h in range(HEADS):
                    rows = slice(DH * (h % 2), DH * (h % 2) + DH)
                    last = nc.tensor.matmul(ps_o[h % 2][:, (h // 2) * P:(h // 2 + 1) * P], wv_in[rows, h // 2, :],
                                            wo_t[rows, h // 2, :], start=True, stop=True)
                last.then_inc(vo_ready, 1)

            def set_up_cols():
                pe.wait_ge(zero_steps, 4)
                for k in range(3):
                    last = nc.tensor.transpose(ps_m[:, k * TC:(k + 1) * TC], rows_in[:, k, :], ident[0:TC, 0:TC])
                last.then_inc(cols_ready, 1)

            def set_up_row(k):
                if k == 0:
                    pe.wait_ge(cols_moved, 1)
                else:
                    pe.wait_ge(rows_moved, k)
                for t in range(4):
                    col = cols[:, k // 2, 4 * (k % 2) + t:4 * (k % 2) + t + 1]
                    last = nc.tensor.transpose(ps_m[:, t * P:(t + 1) * P], col.to_broadcast([P, P]), ident[:])
                last.then_inc(rows_ready, 1)

            def iteration(i, s, do_n, do_a, do_c, do_f):
                n, a, c, f = i + 1, i, i - 1, i - 2

                def three(ps, lhs_hi, lhs_lo, rhs_hi, rhs_lo, start=True, stop=True):
                    nc.tensor.matmul(ps, lhs_lo, rhs_hi, start=start, stop=False)
                    nc.tensor.matmul(ps, lhs_hi, rhs_lo, start=False, stop=False)
                    return nc.tensor.matmul(ps, lhs_hi, rhs_hi, start=False, stop=stop)

                def project_k(j):
                    fc = slice(j * P, (j + 1) * P)
                    if j == 0:
                        pe.wait_ge(chi_done, a + 1)
                        pe.wait_ge(clo_done, a + 1)
                    if begun(4 * a + j):
                        pe.wait_ge(kexp_done, 4 * a + j)
                    for h in range(HALVES):
                        three(halves(ps_k)[h], wk_hi[:, fc], wk_lo[:, fc], halves(c_hi)[h],
                              halves(c_lo)[h]).then_inc(k_ready, 1)

                def project_q(j):
                    tc = slice(j * P, (j + 1) * P)
                    if j == 0:
                        pe.wait_ge(xnhi_done, a + 1)
                        pe.wait_ge(xnlo_done, a + 1)
                    if begun(8 * a + j):
                        pe.wait_ge(qsub_done, 8 * a + j)
                    three(ps_q[:], xn_hi[s][:, tc], xn_lo[s][:, tc], wq_hi[:], wq_lo[:]).then_inc(q_ready, 1)

                def transpose_q(b, j):
                    pe.wait_ge(qs_done, 8 * b + j + 1)
                    if begun(8 * b + j):
                        pe.wait_ge(qlo_done, 8 * b + j)
                    for fc in range(HC):
                        last = nc.tensor.transpose(ps_tb[:, fc * P:(fc + 1) * P],
                                                   q_exp[:, j, fc * P:(fc + 1) * P], ident[:])
                    last.then_inc(tq_ready, 1)

                def transpose_k(k, tq_before):
                    pe.wait_ge(kexp_done, 4 * a + k // 2 + 1)
                    if begun(8 * a + k - 1):
                        pe.wait_ge(tk_moved, 8 * a + k - 1)
                    if k % 2 and begun(tq_before):
                        pe.wait_ge(qlo_done, tq_before)
                    for t in range(4):
                        tok = (4 * (k % 2) + t) * P
                        last = nc.tensor.transpose((ps_ta, ps_tb)[k % 2][:, t * P:(t + 1) * P],
                                                   k_exp[:, (k // 2) % 2, tok:tok + P], ident[:])
                    last.then_inc(tk_ready, 1)

                def mix_m(t0, t1):
                    if t0 == 0:
                        pe.wait_ge(tk_moved, 8 * (c + 1))
                        pe.wait_ge(tc_moved, 2 * (c + 1))
                        if isinstance(i, int) and i == 1:
                            pe.wait_ge(rows_moved, 6)
                        if begun(2 * (c - 1)):
                            pe.wait_ge(ymul_done, 2 * (c - 1))
                    for t in range(t0, t1):
                        last = nc.tensor.matmul(ps_m[:], c_t[:, t, :], k_t[:, t, :], start=(t == 0),
                                                stop=(t == TC - 1))
                    if t1 == TC:
                        last.then_inc(m_ready, 1)

                def mix_g():
                    pe.wait_ge(m_moved, c + 1)
                    if isinstance(i, int) and i == 1:
                        pe.wait_ge(vo_moved, 2)
                    if do_f:
                        pe.wait_ge(x2lo_done, 2 * (f + 1))
                    for h in range(HEADS):
                        rows = slice(DH * (h % 2), DH * (h % 2) + DH)
                        last = nc.tensor.matmul(ps_o[0][rows, (h // 2) * P:(h // 2 + 1) * P],
                                                m_t[:, h * DH:(h + 1) * DH], vo[:, h * P:(h + 1) * P],
                                                start=True, stop=True)
                    last.then_inc(g_ready, 1)

                def mix_out(h, f0, f1):
                    tok = slice(h * BANK, (h + 1) * BANK)
                    if h == 0 and f0 == 0:
                        pe.wait_ge(ghi_done, c + 1)
                        pe.wait_ge(glo_done, c + 1)
                    if f0 == 0:
                        pe.wait_ge(qlo_done, 8 * c + 4 * (h + 1))
                    for fc in range(f0, f1):
                        last = three(ps_o[h][:], g_hi[:, fc, :], g_lo[:, fc, :], q_hi[:, fc, tok], q_lo[:, fc, tok],
                                     start=(fc == 0), stop=(fc == HC - 1))
                    if f1 == HC:
                        last.then_inc(out_ready, 1)

                def feed_forward(h, k0, k1):
                    ps_y = ps_q if h == 1 and not do_a else ps_m
                    for k in range(k0, k1):
                        if k == 0:
                            if h == 0:
                                if isinstance(i, int) and i == 2:
                                    pe.wait_ge(w_converted, 2 * RC)
                                pe.wait_ge(x2hi_done, 2 * (f + 1))
                                pe.wait_ge(x2lo_done, 2 * (f + 1))
                                if do_c:
                                    pe.wait_ge(m_moved, c + 1)
                            elif do_a:
                                pe.wait_ge(ymul_done, 2 * f + 1)
                        w = halves(w_int[:, k // RC, k % RC, :])[h]
                        nc.tensor.matmul(ps_y[:], x2_lo[:, k, :], w, start=(k == 0), stop=False)
                        last = nc.tensor.matmul(ps_y[:], x2_hi[:, k, :], w, start=False, stop=(k == TC - 1))
                    if k1 == TC:
                        last.then_inc(y_ready, 1)

                for j in range(STEPS):
                    if 2 <= j < 6 and do_a:
                        if j == 2 and begun(a - 1):
                            pe.wait_ge(n2_moved, a - 1)
                        transpose_k(2 * (j - 2), 0)
                    if j < HC and do_a:
                        project_k(j)
                    if do_a:
                        project_q(j)
                    if j in (2, 3) and do_a:
                        transpose_k(2 * (j - 2) + 1, 8 * a + j - 4)
                    if j == 2 and do_c:
                        mix_g()
                    if isinstance(i, int) and i == 0:
                        if j == 0:
                            set_up_vo()
                            set_up_cols()
                        elif j < 7:
                            set_up_row(j - 1)
                    if j < 2 and do_c:
                        mix_m(4 * j, 4 * j + 4)
                    if j == 3 and do_c:
                        mix_out(0, 0, 2)
                    if j == 4 and do_f:
                        feed_forward(0, 0, 4)
                    if j == 5 and do_f:
                        feed_forward(0, 4, TC)
                    if j in (4, 5) and do_a:
                        transpose_k(2 * (j - 2) + 1, 8 * a + j - 4)
                    if j == 1 and do_f:
                        pe.wait_ge(x2n_done, f + 1)
                        if do_c:
                            pe.wait_ge(tc_moved, 2 * (c + 1))
                        else:
                            pe.wait_ge(att_done, 2 * (f + 1))
                        for h in range(2):
                            for m in range(RC):
                                last = nc.tensor.transpose(ps_o[h][:, m * P:(m + 1) * P],
                                                           x2n[:, h, m * P:(m + 1) * P], ident[:])
                            last.then_inc(tx_ready, 1)
                    if j == 3 and do_c:
                        mix_out(0, 2, HC)
                    if j == 4 and do_c:
                        mix_out(1, 0, HC)
                    if j == 5 and do_c:
                        pe.wait_ge(sq_done, 2 * (c + 1))
                        if do_a:
                            pe.wait_ge(tk_moved, 8 * a + 7)
                        for t in range(TC):
                            last = nc.tensor.matmul(ps_ta[:, t:t + 1], sq[:, t * P:(t + 1) * P], ones[:],
                                                    start=True, stop=True)
                        last.then_inc(n2_ready, 1)
                    if j == 6 and do_f:
                        feed_forward(1, 0, 3)
                    if j == 6 and do_c:
                        pe.wait_ge(rn_done, c + 1)
                        pe.wait_ge(og_done, 2 * (c + 1))
                        for t in range(TC):
                            last = nc.tensor.transpose(ps_o[t // 4][:, (t % 4) * P:(t % 4 + 1) * P],
                                                       rn[:, t:t + 1].to_broadcast([P, P]), ident[:])
                            if t % 4 == 3:
                                last.then_inc(rb_ready, 1)
                    if j == 7 and do_f:
                        feed_forward(1, 3, TC)
                    if j == 7 and do_a:
                        if isinstance(i, int) and i == 0:
                            pe.wait_ge(vo_moved, 2)
                        if do_c:
                            pe.wait_ge(att_done, 2 * (c + 1))
                        for h in range(2):
                            for t in range(4):
                                tok = (4 * h + t) * P
                                last = nc.tensor.transpose(ps_o[h][:, t * P:(t + 1) * P],
                                                           c_in[s][:, tok:tok + P], ident[:])
                            last.then_inc(tc_ready, 1)
                    if 2 <= j < 6 and do_a:
                        pe.wait_ge(tk_moved, 8 * a + 2 * (j - 2) + 2)
                    if j < 4 and do_c:
                        transpose_q(c, j + 4)
                    if j >= 4 and do_a:
                        transpose_q(a, j - 4)

            pipeline(pe, iteration)



_INS = ["x", "ctx_4096", "L0_xattn_Wq", "L0_xattn_Wk", "L0_xattn_Wv", "L0_xattn_Wo", "L0_xattn_bo", "L0_xattn_g",
        "L0_ffn_qweight", "L0_ffn_scales", "L0_ffn_zeros", "L0_ffn_bias"]


def kernel(**inputs):
    import concourse.bacc as bacc
    from concourse.bass_utils import run_bass_kernel_spmd

    nc = bacc.Bacc("TRN2", target_bir_lowering=False, num_devices=1)
    arrays, args = {}, []
    for name in _INS:
        a = np.ascontiguousarray(inputs[name])
        arrays[f"in_{name}"] = a
        args.append(nc.dram_tensor(f"in_{name}", a.shape, mybir.dt.from_np(a.dtype), kind="ExternalInput").ap())
    out = nc.dram_tensor("out_x", inputs["x"].shape, F32, kind="ExternalOutput").ap()
    build(nc, *args, out)
    r = run_bass_kernel_spmd(nc, [arrays], core_ids=[0])
    return r.results[0]["out_x"]
```
